# Optimizing a Trainium2 kernel written in Bass

```python
import numpy as np
import jax
import jax.numpy as jnp

def _softmax(x, axis=-1):
    return jax.nn.softmax(x, axis=axis)

def _gelu(x):
    return jax.nn.gelu(x, approximate=True)

def _silu(x):
    return jax.nn.silu(x)

def _sigmoid(x):
    return jax.nn.sigmoid(x)

def _layernorm(x, axis=-1, eps=1e-05):
    m = jnp.mean(x, axis=axis, keepdims=True)
    v = jnp.var(x, axis=axis, keepdims=True)
    return (x - m) / jnp.sqrt(v + eps)

def _scatter_add(tgt, idx, src, axis=0):
    return tgt.at[idx].add(src)

def _segment_sum(src, seg, n):
    return jax.ops.segment_sum(src, seg, n)
kernel_name = 'mk_xattn_seq_d2_seqx_r4_68965a'

def setup_inputs(seed: int=0):
    np.random.seed(seed)
    _w = jnp.asarray

    def _rec_inputs():
        import jax
        import jax.numpy as jnp
        _rk = jax.random.key(seed)
        x = -0.000929 + 1 * jax.random.normal(jax.random.fold_in(_rk, 1), (8, 256, 256), jnp.float32)
        _lenS = 256 - jax.random.randint(jax.random.fold_in(_rk, 7), (8,), 0, max(1, 256 // 4) + 1, jnp.int32)
        _lenS2 = 120 - jax.random.randint(jax.random.fold_in(_rk, 8), (8,), 0, max(1, 120 // 4) + 1, jnp.int32)
        _ctx_768P = jax.random.normal(jax.random.fold_in(_rk, 11), (8, 16, 192), jnp.float32)
        _ctx_768c = jax.random.dirichlet(jax.random.fold_in(_rk, 511), 0.3 * jnp.ones((16,), jnp.float32), (8, 120))
        _ctx_768t = jnp.einsum('bsk,bkd->bsd', _ctx_768c, _ctx_768P)
        _ctx_768t = _ctx_768t * jax.lax.rsqrt(jnp.mean(jnp.square(_ctx_768t)) + 1e-12) * 0.953939
        ctx_768 = -5.15168e-05 + 0.999825 * (_ctx_768t + 0.3 * jax.random.normal(jax.random.fold_in(_rk, 611), (8, 120, 192), jnp.float32))
        return (x, ctx_768)
    x, ctx_768 = _rec_inputs()

    def _L0_xattn_setup():
        import jax, jax.numpy as jnp
        import numpy as np
        LN_EPS = 1e-05

        def _ln(x, g, b):
            m = jnp.mean(x, axis=-1, keepdims=True)
            v = jnp.mean((x - m) ** 2, axis=-1, keepdims=True)
            return (x - m) / jnp.sqrt(v + LN_EPS) * g + b
        key = jax.random.key(seed)
        ks = jax.random.split(key, 8)
        B, N, S, D, T = (16, 64, 512, 256, 192)

        def xavier(k, shape):
            fan_in, fan_out = shape
            lim = (6.0 / (fan_in + fan_out)) ** 0.5
            return jax.random.uniform(k, shape, minval=-lim, maxval=lim, dtype=jnp.float32)
        return {'prev_states': jax.random.normal(ks[0], (B, N, D), dtype=jnp.float32), 'input_tokens': jax.random.normal(ks[1], (B, S, T), dtype=jnp.float32), 'W_proj': xavier(ks[2], (T, D)), 'b_proj': jnp.zeros((D,), jnp.float32), 'g_state': jnp.ones((D,), jnp.float32), 'beta_state': jnp.zeros((D,), jnp.float32), 'g_input': jnp.ones((D,), jnp.float32), 'beta_input': jnp.zeros((D,), jnp.float32), 'g_out': jnp.ones((D,), jnp.float32), 'beta_out': jnp.zeros((D,), jnp.float32), 'W_u': xavier(ks[3], (2 * D, D)), 'b_u': jnp.full((D,), -1.0, jnp.float32), 'W_r': xavier(ks[4], (2 * D, D)), 'b_r': jnp.zeros((D,), jnp.float32), 'W_n': xavier(ks[5], (2 * D, D)), 'b_n': jnp.zeros((D,), jnp.float32)}
    _L0_xattn_all = _L0_xattn_setup()
    _L0_xattn_in = {k: v for k, v in _L0_xattn_all.items() if k in ('W_proj', 'b_proj', 'g_state', 'beta_state', 'g_input', 'beta_input', 'g_out', 'beta_out', 'W_u', 'b_u', 'W_r', 'b_r', 'W_n', 'b_n')}
    del _L0_xattn_all

    def _L1_xattn_setup():
        import jax, jax.numpy as jnp
        import numpy as np
        EPS = 1e-05
        HEADS = 16
        D_HEAD = 64
        SCALE = D_HEAD ** (-0.5)

        def layernorm(x, g, b):
            m = jnp.mean(x, axis=-1, keepdims=True)
            v = jnp.var(x, axis=-1, keepdims=True)
            return (x - m) * jax.lax.rsqrt(v + EPS) * g + b

        def attention(x, ctx, Wq, Wk, Wv, Wo, bo):
            b, n, _ = x.shape
            m = ctx.shape[1]
            q = (x @ Wq).reshape(b, n, HEADS, D_HEAD)
            k = (ctx @ Wk).reshape(b, m, HEADS, D_HEAD)
            v = (ctx @ Wv).reshape(b, m, HEADS, D_HEAD)
            sim = jnp.einsum('bihd,bjhd->bhij', q, k) * SCALE
            attn = jax.nn.softmax(sim, axis=-1)
            out = jnp.einsum('bhij,bjhd->bihd', attn, v).reshape(b, n, HEADS * D_HEAD)
            return out @ Wo + bo
        key = jax.random.key(seed)
        ks = jax.random.split(key, 16)
        dim, ctx_dim, inner = (256, 192, HEADS * D_HEAD)
        ff_inner = 4 * dim
        s = lambda k, *sh: jax.random.normal(k, sh, jnp.float32) * 0.02
        return {'x': jax.random.normal(ks[0], (2, 512, dim), jnp.float32), 'context': jax.random.normal(ks[1], (2, 77, ctx_dim), jnp.float32), 'ln1_g': jnp.ones((dim,), jnp.float32), 'ln1_b': jnp.zeros((dim,), jnp.float32), 'a1_Wq': s(ks[2], dim, inner), 'a1_Wk': s(ks[3], dim, inner), 'a1_Wv': s(ks[4], dim, inner), 'a1_Wo': s(ks[5], inner, dim), 'a1_bo': jnp.zeros((dim,), jnp.float32), 'ln2_g': jnp.ones((dim,), jnp.float32), 'ln2_b': jnp.zeros((dim,), jnp.float32), 'a2_Wq': s(ks[6], dim, inner), 'a2_Wk': s(ks[7], ctx_dim, inner), 'a2_Wv': s(ks[8], ctx_dim, inner), 'a2_Wo': s(ks[9], inner, dim), 'a2_bo': jnp.zeros((dim,), jnp.float32), 'ln3_g': jnp.ones((dim,), jnp.float32), 'ln3_b': jnp.zeros((dim,), jnp.float32), 'ff_Wp': s(ks[10], dim, 2 * ff_inner), 'ff_bp': jnp.zeros((2 * ff_inner,), jnp.float32), 'ff_Wo': s(ks[11], ff_inner, dim), 'ff_bo': jnp.zeros((dim,), jnp.float32)}
    _L1_xattn_all = _L1_xattn_setup()
    _L1_xattn_in = {k: v for k, v in _L1_xattn_all.items() if k in ('ln1_g', 'ln1_b', 'a1_Wq', 'a1_Wk', 'a1_Wv', 'a1_Wo', 'a1_bo', 'ln2_g', 'ln2_b', 'a2_Wq', 'a2_Wk', 'a2_Wv', 'a2_Wo', 'a2_bo', 'ln3_g', 'ln3_b', 'ff_Wp', 'ff_bp', 'ff_Wo', 'ff_bo')}
    del _L1_xattn_all
    return {'x': x, 'ctx_768': ctx_768, 'L0_xattn_W_proj': _L0_xattn_in['W_proj'], 'L0_xattn_b_proj': _L0_xattn_in['b_proj'], 'L0_xattn_g_state': _L0_xattn_in['g_state'], 'L0_xattn_beta_state': _L0_xattn_in['beta_state'], 'L0_xattn_g_input': _L0_xattn_in['g_input'], 'L0_xattn_beta_input': _L0_xattn_in['beta_input'], 'L0_xattn_g_out': _L0_xattn_in['g_out'], 'L0_xattn_beta_out': _L0_xattn_in['beta_out'], 'L0_xattn_W_u': _L0_xattn_in['W_u'], 'L0_xattn_b_u': _L0_xattn_in['b_u'], 'L0_xattn_W_r': _L0_xattn_in['W_r'], 'L0_xattn_b_r': _L0_xattn_in['b_r'], 'L0_xattn_W_n': _L0_xattn_in['W_n'], 'L0_xattn_b_n': _L0_xattn_in['b_n'], 'L1_xattn_ln1_g': _L1_xattn_in['ln1_g'], 'L1_xattn_ln1_b': _L1_xattn_in['ln1_b'], 'L1_xattn_a1_Wq': _L1_xattn_in['a1_Wq'], 'L1_xattn_a1_Wk': _L1_xattn_in['a1_Wk'], 'L1_xattn_a1_Wv': _L1_xattn_in['a1_Wv'], 'L1_xattn_a1_Wo': _L1_xattn_in['a1_Wo'], 'L1_xattn_a1_bo': _L1_xattn_in['a1_bo'], 'L1_xattn_ln2_g': _L1_xattn_in['ln2_g'], 'L1_xattn_ln2_b': _L1_xattn_in['ln2_b'], 'L1_xattn_a2_Wq': _L1_xattn_in['a2_Wq'], 'L1_xattn_a2_Wk': _L1_xattn_in['a2_Wk'], 'L1_xattn_a2_Wv': _L1_xattn_in['a2_Wv'], 'L1_xattn_a2_Wo': _L1_xattn_in['a2_Wo'], 'L1_xattn_a2_bo': _L1_xattn_in['a2_bo'], 'L1_xattn_ln3_g': _L1_xattn_in['ln3_g'], 'L1_xattn_ln3_b': _L1_xattn_in['ln3_b'], 'L1_xattn_ff_Wp': _L1_xattn_in['ff_Wp'], 'L1_xattn_ff_bp': _L1_xattn_in['ff_bp'], 'L1_xattn_ff_Wo': _L1_xattn_in['ff_Wo'], 'L1_xattn_ff_bo': _L1_xattn_in['ff_bo']}

def reference(x, ctx_768, L0_xattn_W_proj, L0_xattn_b_proj, L0_xattn_g_state, L0_xattn_beta_state, L0_xattn_g_input, L0_xattn_beta_input, L0_xattn_g_out, L0_xattn_beta_out, L0_xattn_W_u, L0_xattn_b_u, L0_xattn_W_r, L0_xattn_b_r, L0_xattn_W_n, L0_xattn_b_n, L1_xattn_ln1_g, L1_xattn_ln1_b, L1_xattn_a1_Wq, L1_xattn_a1_Wk, L1_xattn_a1_Wv, L1_xattn_a1_Wo, L1_xattn_a1_bo, L1_xattn_ln2_g, L1_xattn_ln2_b, L1_xattn_a2_Wq, L1_xattn_a2_Wk, L1_xattn_a2_Wv, L1_xattn_a2_Wo, L1_xattn_a2_bo, L1_xattn_ln3_g, L1_xattn_ln3_b, L1_xattn_ff_Wp, L1_xattn_ff_bp, L1_xattn_ff_Wo, L1_xattn_ff_bo):
    import jax
    import jax.numpy as jnp

    def _L0_xattn_ref(prev_states, input_tokens, W_proj, b_proj, g_state, beta_state, g_input, beta_input, g_out, beta_out, W_u, b_u, W_r, b_r, W_n, b_n):
        import jax, jax.numpy as jnp
        import numpy as np
        LN_EPS = 1e-05

        def _ln(x, g, b):
            m = jnp.mean(x, axis=-1, keepdims=True)
            v = jnp.mean((x - m) ** 2, axis=-1, keepdims=True)
            return (x - m) / jnp.sqrt(v + LN_EPS) * g + b
        D = prev_states.shape[-1]
        tok = input_tokens @ W_proj + b_proj
        scores = jnp.einsum('bnd,bsd->bns', prev_states, tok) / jnp.sqrt(jnp.float32(D))
        attn = jax.nn.softmax(scores, axis=-1)
        routed = jnp.einsum('bns,bsd->bnd', attn, tok)
        ps_n = _ln(prev_states, g_state, beta_state)
        in_n = _ln(routed, g_input, beta_input)
        concat = jnp.concatenate([ps_n, in_n], axis=-1)
        u = jax.nn.sigmoid(concat @ W_u + b_u)
        r = jax.nn.sigmoid(concat @ W_r + b_r)
        reset_in = jnp.concatenate([r * ps_n, in_n], axis=-1)
        cand = jnp.tanh(reset_in @ W_n + b_n)
        new_state = (1.0 - u) * prev_states + u * cand
        return _ln(new_state, g_out, beta_out)

    def _L1_xattn_ref(x, context, ln1_g, ln1_b, a1_Wq, a1_Wk, a1_Wv, a1_Wo, a1_bo, ln2_g, ln2_b, a2_Wq, a2_Wk, a2_Wv, a2_Wo, a2_bo, ln3_g, ln3_b, ff_Wp, ff_bp, ff_Wo, ff_bo):
        import jax, jax.numpy as jnp
        import numpy as np
        EPS = 1e-05
        HEADS = 16
        D_HEAD = 64
        SCALE = D_HEAD ** (-0.5)

        def layernorm(x, g, b):
            m = jnp.mean(x, axis=-1, keepdims=True)
            v = jnp.var(x, axis=-1, keepdims=True)
            return (x - m) * jax.lax.rsqrt(v + EPS) * g + b

        def attention(x, ctx, Wq, Wk, Wv, Wo, bo):
            b, n, _ = x.shape
            m = ctx.shape[1]
            q = (x @ Wq).reshape(b, n, HEADS, D_HEAD)
            k = (ctx @ Wk).reshape(b, m, HEADS, D_HEAD)
            v = (ctx @ Wv).reshape(b, m, HEADS, D_HEAD)
            sim = jnp.einsum('bihd,bjhd->bhij', q, k) * SCALE
            attn = jax.nn.softmax(sim, axis=-1)
            out = jnp.einsum('bhij,bjhd->bihd', attn, v).reshape(b, n, HEADS * D_HEAD)
            return out @ Wo + bo
        h = layernorm(x, ln1_g, ln1_b)
        x = attention(h, h, a1_Wq, a1_Wk, a1_Wv, a1_Wo, a1_bo) + x
        h = layernorm(x, ln2_g, ln2_b)
        x = attention(h, context, a2_Wq, a2_Wk, a2_Wv, a2_Wo, a2_bo) + x
        h = layernorm(x, ln3_g, ln3_b)
        p = h @ ff_Wp + ff_bp
        u, gate = jnp.split(p, 2, axis=-1)
        ff = u * jax.nn.gelu(gate, approximate=False) @ ff_Wo + ff_bo
        return ff + x
    x = _L0_xattn_ref(x, ctx_768, L0_xattn_W_proj, L0_xattn_b_proj, L0_xattn_g_state, L0_xattn_beta_state, L0_xattn_g_input, L0_xattn_beta_input, L0_xattn_g_out, L0_xattn_beta_out, L0_xattn_W_u, L0_xattn_b_u, L0_xattn_W_r, L0_xattn_b_r, L0_xattn_W_n, L0_xattn_b_n)
    x = _L1_xattn_ref(x, ctx_768, L1_xattn_ln1_g, L1_xattn_ln1_b, L1_xattn_a1_Wq, L1_xattn_a1_Wk, L1_xattn_a1_Wv, L1_xattn_a1_Wo, L1_xattn_a1_bo, L1_xattn_ln2_g, L1_xattn_ln2_b, L1_xattn_a2_Wq, L1_xattn_a2_Wk, L1_xattn_a2_Wv, L1_xattn_a2_Wo, L1_xattn_a2_bo, L1_xattn_ln3_g, L1_xattn_ln3_b, L1_xattn_ff_Wp, L1_xattn_ff_bp, L1_xattn_ff_Wo, L1_xattn_ff_bo)
    return x

_drawn_inputs = setup_inputs


def setup_inputs(seed=0):
    import zlib

    import numpy as np

    out = dict(_drawn_inputs(seed))
    spreads = {'L0_xattn_b_proj': (0.0, 0.1),
     'L0_xattn_g_state': (1.0, 0.2),
     'L0_xattn_beta_state': (0.0, 0.277),
     'L0_xattn_g_input': (1.0, 0.2),
     'L0_xattn_beta_input': (0.0, 0.1),
     'L0_xattn_g_out': (1.0, 0.2),
     'L0_xattn_beta_out': (0.0, 0.1),
     'L0_xattn_b_u': (-1.0, 0.2),
     'L0_xattn_b_r': (0.0, 0.8),
     'L0_xattn_b_n': (0.0, 0.1),
     'L1_xattn_ln1_g': (1.0, 0.6),
     'L1_xattn_ln1_b': (0.0, 0.399),
     'L1_xattn_a1_bo': (0.0, 0.1),
     'L1_xattn_ln2_g': (1.0, 0.6),
     'L1_xattn_ln2_b': (0.0, 0.8),
     'L1_xattn_a2_bo': (0.0, 0.1),
     'L1_xattn_ln3_g': (1.0, 0.6),
     'L1_xattn_ln3_b': (0.0, 0.8),
     'L1_xattn_ff_bp': (0.0, 0.508),
     'L1_xattn_ff_bo': (0.0, 0.1)}
    factors = {'L1_xattn_a1_Wq': 8.0, 'L1_xattn_a1_Wk': 8.0, 'L1_xattn_a2_Wq': 8.0, 'L1_xattn_a2_Wk': 8.0}
    for name, (base, spread) in spreads.items():
        noise = np.random.default_rng([zlib.crc32(name.encode()), seed]).standard_normal(out[name].shape)
        drawn = base * np.exp(spread * noise) if base else spread * noise
        out[name] = jnp.asarray(drawn.astype(out[name].dtype))
    for name, factor in factors.items():
        out[name] = (out[name] * factor).astype(out[name].dtype)
    return out
```

```python
from contextlib import ExitStack

import concourse.bass as bass
from concourse import mybir

F32 = mybir.dt.float32
F32R = mybir.dt.float32r
ALU = mybir.AluOpType
ACT = mybir.ActivationFunctionType
AX = mybir.AxisListType

B, S, D = 8, 256, 256
SC, DC = 120, 192
HEADS, DH = 16, 64
PAIRS = HEADS // 2
FF = 1024
KT = D // 128
NT = S // 128
EPS = 1e-5
L0B = 2
L0T = L0B * NT
CH = 1024
STAGES = 4
VW = 3 * DH

PCOLS = ["L0_xattn_g_state", "L0_xattn_beta_state", "L0_xattn_g_input", "L0_xattn_beta_input",
         "L0_xattn_b_u", "L0_xattn_b_r", "L0_xattn_b_n", "L0_xattn_b_proj",
         "L1_xattn_ln1_g", "L1_xattn_ln1_b", "L1_xattn_ln2_g", "L1_xattn_ln2_b",
         "L1_xattn_ln3_g", "L1_xattn_ln3_b"]
NPC = KT * len(PCOLS) + 2 * FF // 128
ROWS = ["L0_xattn_b_proj", "L0_xattn_g_out", "L0_xattn_beta_out", "L1_xattn_a1_bo", "L1_xattn_a2_bo", "L1_xattn_ff_bo"]
WSETS = [["L0_xattn_W_proj", "L0_xattn_W_r", "L0_xattn_W_u", "L0_xattn_W_n"],
         ["L1_xattn_a1_Wq", "L1_xattn_a1_Wk", "L1_xattn_a1_Wv", "L1_xattn_a1_Wo"],
         ["L1_xattn_a2_Wq", "L1_xattn_a2_Wk", "L1_xattn_a2_Wv", "L1_xattn_a2_Wo"],
         ["L1_xattn_ff_Wp", "L1_xattn_ff_Wo"]]
KTILES = {"L0_xattn_W_proj": 2, "L0_xattn_W_r": 4, "L0_xattn_W_u": 4, "L0_xattn_W_n": 4,
          "L1_xattn_a1_Wq": 2, "L1_xattn_a1_Wk": 2, "L1_xattn_a1_Wv": 2, "L1_xattn_a1_Wo": PAIRS,
          "L1_xattn_a2_Wq": 2, "L1_xattn_a2_Wk": 2, "L1_xattn_a2_Wv": 2, "L1_xattn_a2_Wo": PAIRS,
          "L1_xattn_ff_Wp": 2, "L1_xattn_ff_Wo": FF // 128}
NCOL = {w: D if w.startswith("L0") or w.endswith("Wo") else 2 * FF if w.endswith("Wp") else HEADS * DH for w in KTILES}
WIDTH = {w: KTILES[w] * NCOL[w] for w in KTILES}
WCHUNKS = [-(-sum(WIDTH[w] for w in ws) // CH) for ws in WSETS]
QCHUNKS = KT * HEADS * DH // CH


def build(nc, x, ctx_p, weights, params, rows, ident_in, x1_dram, x2_dram, x3_dram, out):
    es = ExitStack()
    with es:
        def sb(name, shape, dt=F32, where=es):
            return where.enter_context(nc.sbuf_tensor(name, shape, dt))

        def sem(name):
            return es.enter_context(nc.semaphore(name))

        WH = sb("w_hi", [128, 8 * CH], F32R)
        WL = sb("w_lo", [128, 8 * CH], F32R)
        stage = sb("w_stage", [128, STAGES, CH])
        pp = sb("params_pp", [128, NPC])
        rb = sb("rows_bc", [128, len(ROWS), D])
        ident = sb("ident", [128, 128])
        neg_half = sb("neg_half", [128, L0T])
        half_b = sb("half_b", [128, 2 * KT])
        mv = sb("mean_var", [128, L0T, 2])
        mv2 = sb("mean_var2", [128, L0T, 2])
        st6 = sb("bn6", [128, L0T, 6])
        rstd = sb("rstd", [128, L0T])
        rstd2 = sb("rstd2", [128, L0T])

        def pcol(name, kt):
            i = KT * PCOLS.index(name) + kt
            return pp[:, i:i + 1]

        def row(name):
            return rb[:, ROWS.index(name), :]

        with ExitStack() as l0:
            x0 = sb("l0_x", [128, L0T, D], where=l0)
            c0 = sb("l0_ctx", [SC, L0B, D], where=l0)
            xTf = sb("l0_xT", [128, KT, L0T * 128], where=l0)
            xTh = sb("l0_xT_hi", [128, KT, L0T * 128], F32R, where=l0)
            xTl = sb("l0_xT_lo", [128, KT, L0T * 128], F32R, where=l0)
            cTh = sb("l0_cT_hi", [128, KT, L0B * SC], F32R, where=l0)
            cTl = sb("l0_cT_lo", [128, KT, L0B * SC], F32R, where=l0)
            tTh = sb("l0_tokT_hi", [128, KT, L0B * SC], F32R, where=l0)
            tTl = sb("l0_tokT_lo", [128, KT, L0B * SC], F32R, where=l0)
            tkf = sb("l0_tok", [SC, L0B, D], where=l0)
            tkh = sb("l0_tok_hi", [SC, L0B, D], F32R, where=l0)
            tkl = sb("l0_tok_lo", [SC, L0B, D], F32R, where=l0)
            nm0 = sb("l0_negmax", [128, L0T], where=l0)
            nms0 = sb("l0_negmax_scaled", [128, L0T], where=l0)
            sum0 = sb("l0_sum", [128, L0T], where=l0)
            rs0 = sb("l0_rsum", [128, L0T], where=l0)
            p0 = sb("l0_p", [128, L0T, SC], where=l0)
            pTh0 = sb("l0_pT_hi", [SC, L0T * 128], F32R, where=l0)
            pTl0 = sb("l0_pT_lo", [SC, L0T * 128], F32R, where=l0)
            rt = sb("l0_routed", [128, L0T, D], where=l0)
            xh0 = sb("l0_xhat", [128, L0T, D], where=l0)
            psf = sb("l0_psT", [128, KT, L0T * 128], where=l0)
            psh = sb("l0_psT_hi", [128, KT, L0T * 128], F32R, where=l0)
            psl = sb("l0_psT_lo", [128, KT, L0T * 128], F32R, where=l0)
            inf = sb("l0_inT", [128, KT, L0T * 128], where=l0)
            inh = sb("l0_inT_hi", [128, KT, L0T * 128], F32R, where=l0)
            inl = sb("l0_inT_lo", [128, KT, L0T * 128], F32R, where=l0)
            tr = sb("l0_tanh_r", [128, KT, L0T * 128], where=l0)
            rph = sb("l0_rps_hi", [128, KT, L0T * 128], F32R, where=l0)
            rpl = sb("l0_rps_lo", [128, KT, L0T * 128], F32R, where=l0)
            tu = sb("l0_tanh_u", [128, KT, L0T * 128], where=l0)
            cand = sb("l0_cand", [128, KT, L0T * 128], where=l0)

        with ExitStack() as l1:
            xin = sb("x_in", [128, NT, D], where=l1)
            xhat = sb("xhat", [128, NT, D], where=l1)
            xb = sb("x_plus_bias", [128, NT, D], where=l1)
            hf = sb("hT", [128, KT, S], where=l1)
            hh = sb("hT_hi", [128, KT, S], F32R, where=l1)
            hl = sb("hT_lo", [128, KT, S], F32R, where=l1)
            xo = sb("x_out", [128, NT, D], where=l1)
            with ExitStack() as att:
                qkh = sb("qkT_hi", [128, PAIRS, 2, S], F32R, where=att)
                qkl = sb("qkT_lo", [128, PAIRS, 2, S], F32R, where=att)
                vh = sb("v_hi", [128, NT, PAIRS * VW], F32R, where=att)
                vl = sb("v_lo", [128, NT, PAIRS * VW], F32R, where=att)
                p = sb("p", [128, 2, 2, NT * S], where=att)
                pTh = sb("pT_hi", [128, 2, 2, NT * S], F32R, where=att)
                pTl = sb("pT_lo", [128, 2, 2, NT * S], F32R, where=att)
                negmax = sb("negmax", [128, 2, NT, 2], where=att)
                expsum = sb("expsum", [128, 2, NT, 2], where=att)
                rs = sb("rsum", [128, 2, NT, 2], where=att)
                rsb = sb("rsum_wide", [128, 2, NT, 2 * DH], where=att)
                rT = sb("rsumT", [128, S], where=att)
                of = sb("oT", [128, S], where=att)
                oh = sb("oT_hi", [128, PAIRS, S], F32R, where=att)
                ol = sb("oT_lo", [128, PAIRS, S], F32R, where=att)
                cin = sb("ctx_in", [SC, D], where=att)
                ch = sb("cT_hi", [128, KT, SC], F32R, where=att)
                cl = sb("cT_lo", [128, KT, SC], F32R, where=att)
            kdh = qkh[:, :, 1, 0:2 * SC]
            kdl = qkl[:, :, 1, 0:2 * SC]
            with ExitStack() as ff:
                gl = sb("gelu", [128, 2, S], where=ff)
                fu = sb("ff_f", [128, 2, S], where=ff)
                fh = sb("ffT_hi", [128, FF // 128, S], F32R, where=ff)
                fl = sb("ffT_lo", [128, FF // 128, S], F32R, where=ff)

        bank = [es.enter_context(nc.psum_tensor(f"bank{i}", [128, 512], F32)) for i in range(8)]

        consts_in = sem("consts_in")
        passed = sem("passed")
        neg_half_ready = sem("neg_half_ready")
        half_b_ready = sem("half_b_ready")
        zeros_ready = sem("zeros_ready")
        staged = [sem(f"weights_staged{i}") for i in range(STAGES)]
        w_hi_ready = sem("w_hi_ready")
        w_ready = sem("w_ready")
        z = {n: sem("l0_" + n) for n in (
            "in", "xT", "cT", "xT_full", "xT_hi", "xT_split", "cT_hi", "cT_split", "stats", "rstd", "xhat",
            "tokT", "tok", "tokT_hi", "tokT_split", "tok_full", "tok_hi", "tok_split", "scores", "negmax", "exp",
            "rsum", "pT", "pT_hi", "pT_split", "routed", "rt", "rstats", "rrstd", "rhat", "psT", "ps_full", "ps_hi",
            "ps_split", "inT", "in_full", "in_hi", "in_split", "gate_r", "tanh_r", "rps", "rps_hi", "rps_split",
            "gate_u", "tanh_u", "gate_n", "cand", "new", "new_step", "new_tok", "ostats", "orstd", "ohat", "out",
            "stored")}

        def phase_sems(tag, names):
            return {n: sem(f"{tag}_{n}") for n in names}

        LN = ("in", "xb", "stats", "rstd", "xhat", "hT", "h_full", "h_hi", "h_split", "out", "stored")
        AT = LN + ("qk", "qk_hi", "qk_lo", "v", "v_hi", "v_lo", "scores", "negmax", "exp", "rsum", "rsum_wide", "pT", "pT_hi",
                   "pT_lo", "rT", "rT_copied", "o", "o_norm", "o_hi", "o_lo", "wo", "c_in", "cT", "cT_hi", "cT_lo")
        a1 = phase_sems("a1", AT)
        a2 = phase_sems("a2", AT)
        f3 = phase_sems("ff", LN + ("up", "gelu", "glu", "f_hi", "f_lo", "down"))
        NI = B // L0B
        WBASE = [sum(WCHUNKS[:i]) for i in range(5)]

        def wcols(phase, name, kt, lo_col, n):
            base = 0
            for w in WSETS[phase]:
                if w == name:
                    break
                base += WIDTH[w]
            a = base + kt * NCOL[name] + lo_col
            return WH[:, a:a + n], WL[:, a:a + n]

        def load_weights(sp, phase, first, last):
            for c in range(first, last):
                n = WBASE[phase] + c
                if n >= STAGES:
                    sp.wait_ge(w_ready, n - STAGES + 1)
                sp.dma_start(stage[:, n % STAGES, :], weights[n]).then_inc(staged[n % STAGES], 16)

        def weights_hi(act, phase):
            for c in range(WCHUNKS[phase]):
                n = WBASE[phase] + c
                act.wait_ge(staged[n % STAGES], 16 * (n // STAGES + 1))
                src = stage[:, n % STAGES, :]
                dst = WH[:, c * CH:(c + 1) * CH]
                if phase in (1, 2) and c < QCHUNKS:
                    nc.scalar.mul(dst, src, DH ** -0.5).then_inc(w_hi_ready, 1)
                else:
                    nc.scalar.copy(dst, src).then_inc(w_hi_ready, 1)

        def weights_lo(dve, phase):
            for c in range(WCHUNKS[phase]):
                n = WBASE[phase] + c
                dve.wait_ge(staged[n % STAGES], 16 * (n // STAGES + 1))
                dve.wait_ge(w_hi_ready, n + 1)
                src = stage[:, n % STAGES, :]
                hi = WH[:, c * CH:(c + 1) * CH].bitcast(F32)
                dst = WL[:, c * CH:(c + 1) * CH]
                if phase in (1, 2) and c < QCHUNKS:
                    nc.vector.scalar_tensor_tensor(out=dst, in0=src, scalar=DH ** -0.5, in1=hi,
                                                   op0=ALU.mult, op1=ALU.subtract).then_inc(w_ready, 1)
                else:
                    nc.vector.tensor_tensor(dst, src, hi, ALU.subtract).then_inc(w_ready, 1)

        def v_src(r, c):
            return bank[4 + c if r == 128 else c][0:r, :].rearrange("p (g e d) -> p g e d", g=4, e=2)

        def v_dst(buf, r, c):
            half = slice(c % 2 * 4 * VW, (c % 2 + 1) * 4 * VW)
            return buf[0:r, c // 2, half].rearrange("p (g s d) -> p g s d", g=4, s=3)[:, :, 0:3:2, :]

        def c_src():
            return bank[6][:, :].rearrange("p (k n) -> p k n", k=KT)[:, :, 0:SC]

        def k_src(c, e):
            return bank[2 + c][e * DH:(e + 1) * DH, 0:4 * SC].rearrange("p (g n) -> p g n", g=4)

        def k_dst(buf, c, e):
            return buf[e * DH:(e + 1) * DH, 4 * c:4 * c + 4, e * SC:(e + 1) * SC]

        def q_src(c):
            return bank[4 + c][:, :].rearrange("p (g n) -> p g n", g=2)

        def scores_at(cols, g, e, t):
            if cols == S:
                return bank[g % 2 * 2 + e][:, t * S:(t + 1) * S]
            return bank[g % 4][:, t * S + e * SC:t * S + (e + 1) * SC]

        def apart(engine):
            engine.sem_inc(passed, 1)

        block = es.enter_context(nc.Block())

        @block.sync
        def _(sp):
            for a in (z, a1, a2, f3):
                sp.sem_inc(a["out"], 1)
                sp.sem_inc(a["stored"], 16)
            sp.dma_start(pp[:, :], params).then_inc(consts_in, 16)
            sp.dma_start(ident[:, :], ident_in).then_inc(consts_in, 16)
            for i in range(len(ROWS)):
                sp.dma_start(rb[:, i, :], rows[i:i + 1, :].partition_broadcast(128)).then_inc(consts_in, 16)
            def batches(dram, first, n):
                return dram[bass.ds(first, n), :, :].rearrange("b (t p) d -> p (b t) d", p=128)

            def load_first(it):
                sp.dma_start(x0[:, :, :], batches(x, it * L0B, L0B)).then_inc(z["in"], 16)
                csrc = ctx_p[bass.ds(it * L0B, L0B), :, :].rearrange("b s d -> s b d")
                sp.dma_start(c0[:, :, :], csrc).then_inc(z["in"], 16)

            def store_first(it):
                sp.wait_ge(z["out"], it + 2)
                apart(sp)
                sp.dma_start(batches(x1_dram, it * L0B, L0B), xh0[:, :, :]).then_inc(z["stored"], 16)

            load_first(0)
            load_weights(sp, 0, 0, WCHUNKS[0])
            load_weights(sp, 1, 0, STAGES)
            with sp.Fori(0, NI - 1) as it:
                sp.wait_ge(z["xT"], it + 1)
                apart(sp)
                sp.wait_ge(z["cT"], it + 1)
                apart(sp)
                sp.wait_ge(z["xhat"], (it + 1) * L0T)
                apart(sp)
                load_first(it + 1)
                store_first(it)
            store_first(NI - 1)
            sp.wait_ge(z["stored"], 16 * (NI + 1))
            apart(sp)

            def phase_io(a, phase, src, dst):
                def load(it):
                    sp.dma_start(xin[:, :, :], batches(src, it, 1)).then_inc(a["in"], 16)
                    if phase == 2:
                        sp.dma_start(cin[:, :], ctx_p[bass.ds(it, 1), :, :].rearrange("b s d -> (b s) d")
                                     ).then_inc(a["c_in"], 16)

                def store(it):
                    sp.wait_ge(a["out"], it + 2)
                    apart(sp)
                    sp.dma_start(batches(dst, it, 1), xo[:, :, :]).then_inc(a["stored"], 16)

                load(0)
                load_weights(sp, phase, STAGES, WCHUNKS[phase])
                if phase < 3:
                    load_weights(sp, phase + 1, 0, STAGES)
                with sp.Fori(0, B - 1) as it:
                    sp.wait_ge(a["xb"], it + 1)
                    apart(sp)
                    sp.wait_ge(a["xhat"], (it + 1) * NT)
                    apart(sp)
                    if phase == 2:
                        sp.wait_ge(a["cT"], it + 1)
                        apart(sp)
                    load(it + 1)
                    store(it)
                store(B - 1)
                sp.wait_ge(a["stored"], 16 * (B + 1))
                apart(sp)

            phase_io(a1, 1, x1_dram, x2_dram)
            phase_io(a2, 2, x2_dram, x3_dram)
            phase_io(f3, 3, x3_dram, out)

        @block.gpsimd
        def _(pool):
            nc.gpsimd.memset(neg_half[:, :], -0.5).then_inc(neg_half_ready, 1)
            pool.wait_ge(neg_half_ready, 1)

            def inverse_std(dst, src, n, waited, count, done):
                pool.wait_ge(waited, count)
                nc.gpsimd.tensor_tensor(dst[:, 0:n], src[:, 0:n, 1], neg_half[:, 0:n], ALU.pow).then_inc(done, 1)

            with pool.Fori(0, NI) as it:
                inverse_std(rstd, mv, L0T, z["stats"], (it + 1) * 3 * L0T, z["rstd"])
                inverse_std(rstd2, mv2, L0T, z["rstats"], (it + 1) * 3 * L0T, z["rrstd"])
                inverse_std(rstd, mv, L0T, z["ostats"], (it + 1) * 3 * L0T, z["orstd"])

            def layernorm_and_bias(a, it, bias):
                pool.wait_ge(a["in"], (it + 1) * 16)
                pool.wait_ge(a["out"], it + 1)
                nc.gpsimd.tensor_tensor(xb[:, :, :], xin[:, :, :],
                                        row(bias).unsqueeze(1).broadcast_to([128, NT, D]), ALU.add).then_inc(a["xb"], 1)
                inverse_std(rstd, mv, NT, a["stats"], (it + 1) * 3 * NT, a["rstd"])

            def attention_splits(a, bias):
                with pool.Fori(0, B) as it:
                    layernorm_and_bias(a, it, bias)
                    for s in range(PAIRS + 1):
                        if s < PAIRS:
                            pool.wait_ge(a["rsum"], it * PAIRS + s + 1)
                            apart(pool)
                            nc.gpsimd.tensor_copy(rsb[:, s % 2, :, :].rearrange("p t (e d) -> p (t e) d", e=2),
                                                  rs[:, s % 2, :, :].rearrange("p t e -> p (t e)").unsqueeze(2)
                                                  .broadcast_to([128, NT * 2, DH])).then_inc(a["rsum_wide"], 1)
                        if s == 0:
                            continue
                        g = s - 1
                        pool.wait_ge(a["o_norm"], it * PAIRS + g + 1)
                        apart(pool)
                        nc.gpsimd.tensor_copy(oh[:, g, :], of[:, :]).then_inc(a["o_hi"], 1)
                        pool.wait_ge(a["o_hi"], it * PAIRS + g + 1)
                        nc.gpsimd.tensor_tensor(ol[:, g, :], of[:, :], oh[:, g, :].bitcast(F32),
                                                ALU.subtract).then_inc(a["o_lo"], 1)

            attention_splits(a1, "L1_xattn_a1_bo")
            attention_splits(a2, "L1_xattn_a2_bo")
            with pool.Fori(0, B) as it:
                layernorm_and_bias(f3, it, "L1_xattn_ff_bo")

        @block.scalar
        def _(act):
            act.wait_ge(consts_in, 16 * (2 + len(ROWS)))
            iu = KT * PCOLS.index("L0_xattn_b_u")
            nc.scalar.mul(half_b[:, :], pp[:, iu:iu + 2 * KT], 0.5).then_inc(half_b_ready, 1)
            act.wait_ge(half_b_ready, 1)
            weights_hi(act, 0)
            with act.Fori(0, NI) as it:
                act.wait_ge(z["out"], it + 1)
                act.wait_ge(z["xT"], it + 1)
                for kt in range(KT):
                    nc.scalar.copy(xTh[:, kt, :], bank[kt][:, :])
                    last = nc.scalar.copy(xTf[:, kt, :], bank[kt][:, :])
                last.then_inc(z["xT_hi"], 1)
                act.wait_ge(z["cT"], it + 1)
                cps = bank[2][:, :].rearrange("p (k n) -> p k n", k=KT)[:, :, 0:L0B * SC]
                nc.scalar.copy(cTh[:, :, :], cps).then_inc(z["cT_hi"], 1)
                act.wait_ge(z["tokT"], it + 1)
                tps = bank[3][:, :].rearrange("p (k n) -> p k n", k=KT)[:, :, 0:L0B * SC]
                for m in range(KT):
                    last = nc.scalar.activation(tTh[:, m, :], tps[:, m, :], ACT.Identity,
                                                bias=pcol("L0_xattn_b_proj", m))
                last.then_inc(z["tokT_hi"], 1)
                act.wait_ge(z["tok_full"], it + 1)
                nc.scalar.copy(tkh[:, :, :], tkf[:, :, :]).then_inc(z["tok_hi"], 1)
                act.wait_ge(z["ps_full"], it + 1)
                nc.scalar.copy(psh[:, :, :], psf[:, :, :]).then_inc(z["ps_hi"], 1)
                act.wait_ge(z["negmax"], 2 * (it + 1))
                for t in range(L0T):
                    last = nc.scalar.activation(p0[:, t, :], bank[5][:, t * 128:t * 128 + SC], ACT.Exp,
                                                bias=nms0[:, t:t + 1], scale=D ** -0.5, accum_out=sum0[:, t:t + 1])
                last.then_inc(z["exp"], 1)
                act.wait_ge(z["pT"], it + 1)
                nc.scalar.copy(pTh0[:, :], bank[6][0:SC, :]).then_inc(z["pT_hi"], 1)
                act.wait_ge(z["in_full"], it + 1)
                nc.scalar.copy(inh[:, :, :], inf[:, :, :]).then_inc(z["in_hi"], 1)
                for m in range(KT):
                    act.wait_ge(z["gate_r"], it * KT + m + 1)
                    nc.scalar.activation(tr[:, m, :], bank[5 + m][:, :], ACT.Tanh, bias=half_b[:, KT + m:KT + m + 1],
                                         scale=0.5).then_inc(z["tanh_r"], 1)
                for m in range(KT):
                    act.wait_ge(z["rps"], it * KT + m + 1)
                    nc.scalar.mul(rph[:, m, :], tr[:, m, :], 0.5).then_inc(z["rps_hi"], 1)
                for m in range(KT):
                    act.wait_ge(z["gate_u"], it * KT + m + 1)
                    nc.scalar.activation(tu[:, m, :], bank[(7 + m) % 8][:, :], ACT.Tanh, bias=half_b[:, m:m + 1],
                                         scale=0.5).then_inc(z["tanh_u"], 1)
                for m in range(KT):
                    act.wait_ge(z["gate_n"], it * KT + m + 1)
                    nc.scalar.activation(cand[:, m, :], bank[1 + m][:, :], ACT.Tanh,
                                         bias=pcol("L0_xattn_b_n", m)).then_inc(z["cand"], 1)

            def layernorm(a, it):
                act.wait_ge(a["h_full"], (it + 1) * KT)
                act.wait_ge(a["out"], it + 1)
                nc.scalar.copy(hh[:, :, :], hf[:, :, :]).then_inc(a["h_hi"], 1)

            def softmax_pair(a, it, g, cols):
                for e in range(2):
                    per = 2 if cols == S else 1
                    act.wait_ge(a["negmax"], (it * PAIRS + g) * per + min(e + 1, per))
                    for t in range(NT):
                        last = nc.scalar.activation(p[:, g % 2, e, t * cols:(t + 1) * cols],
                                                    scores_at(cols, g, e, t), ACT.Exp,
                                                    bias=negmax[:, g % 2, t, e:e + 1],
                                                    accum_out=expsum[:, g % 2, t, e:e + 1])
                    last.then_inc(a["exp"], 1)

            def attention(a, it, cols):
                for s in range(PAIRS + 2):
                    if s < PAIRS:
                        softmax_pair(a, it, s, cols)
                    if 1 <= s <= PAIRS:
                        g = s - 1
                        for e in range(2):
                            act.wait_ge(a["pT"], it * HEADS + 2 * g + e + 1)
                            r, n = (128, NT * S) if cols == S else (SC, S)
                            nc.scalar.copy(pTh[0:r, g % 2, e, 0:n], bank[4 + e][0:r, 0:n]).then_inc(a["pT_hi"], 1)
                    if s >= 2:
                        g = s - 2
                        act.wait_ge(a["o"], it * PAIRS + g + 1)
                        nc.scalar.copy(rT[:, :], bank[6][:, S:2 * S]).then_inc(a["rT_copied"], 1)

            act.wait_ge(z["out"], NI + 1)
            weights_hi(act, 1)
            with act.Fori(0, B) as it:
                layernorm(a1, it)
                for g in range(PAIRS):
                    act.wait_ge(a1["qk"], it * PAIRS + g + 1)
                    nc.scalar.copy(qkh[:, g, :, :], bank[g % 4][:, :].rearrange("p (a n) -> p a n", a=2)
                                   ).then_inc(a1["qk_hi"], 1)
                for c in range(4):
                    act.wait_ge(a1["v"], it * 4 + c + 1)
                    nc.scalar.copy(v_dst(vh, 128, c), v_src(128, c)).then_inc(a1["v_hi"], 1)
                attention(a1, it, S)
            act.wait_ge(a1["out"], B + 1)
            weights_hi(act, 2)
            with act.Fori(0, B) as it:
                act.wait_ge(a2["cT"], it + 1)
                act.wait_ge(a2["out"], it + 1)
                nc.scalar.copy(ch[:, :, :], c_src()).then_inc(a2["cT_hi"], 1)
                layernorm(a2, it)
                for c in range(2):
                    act.wait_ge(a2["v"], it * 2 + c + 1)
                    nc.scalar.copy(v_dst(vh, SC, c), v_src(SC, c)).then_inc(a2["v_hi"], 1)
                for c in range(2):
                    act.wait_ge(a2["qk"], it * 6 + c + 1)
                    for e in range(2):
                        last = nc.scalar.copy(k_dst(kdh, c, e), k_src(c, e))
                    last.then_inc(a2["qk_hi"], 1)
                for c in range(4):
                    act.wait_ge(a2["qk"], it * 6 + 3 + c)
                    nc.scalar.copy(qkh[:, 2 * c:2 * c + 2, 0, :], q_src(c)).then_inc(a2["qk_hi"], 1)
                attention(a2, it, SC)
            act.wait_ge(a2["out"], B + 1)
            weights_hi(act, 3)
            with act.Fori(0, B) as it:
                layernorm(f3, it)
                for j in range(FF // 128):
                    act.wait_ge(f3["up"], it * 8 + j + 1)
                    if j >= 2:
                        act.wait_ge(f3["glu"], it * 8 + j - 1)
                    nc.scalar.activation(gl[:, j % 2, :], bank[j % 4][:, S:2 * S], ACT.Gelu,
                                         bias=pp[:, NPC - 8 + j:NPC - 7 + j]).then_inc(f3["gelu"], 1)
                    if j >= 1:
                        act.wait_ge(f3["glu"], it * 8 + j)
                        nc.scalar.copy(fh[:, j - 1, :], fu[:, (j - 1) % 2, :]).then_inc(f3["f_hi"], 1)
                act.wait_ge(f3["glu"], it * 8 + 8)
                nc.scalar.copy(fh[:, 7, :], fu[:, 1, :]).then_inc(f3["f_hi"], 1)

        @block.vector
        def _(dve):
            dve.wait_ge(consts_in, 16 * (2 + len(ROWS)))
            weights_lo(dve, 0)

            def statistics(src, dst, n, sm, base):
                for t in range(n):
                    nc.vector.bn_stats(st6[:, t, :], src(t)).then_inc(sm, 1)
                dve.wait_ge(sm, base + n)
                apart(dve)
                for t in range(n):
                    nc.vector.bn_aggr(dst[:, t, :], st6[:, t, :]).then_inc(sm, 1)
                dve.wait_ge(sm, base + 2 * n)
                for t in range(n):
                    nc.vector.tensor_scalar(dst[:, t, 1:2], dst[:, t, 1:2], EPS, None, ALU.add).then_inc(sm, 1)

            def normalise(dst, src, stat, inv, n, done):
                for t in range(n):
                    nc.vector.tensor_scalar(dst(t), src(t), stat[:, t, 0:1], inv[:, t:t + 1],
                                            ALU.subtract, ALU.mult).then_inc(done, 1)

            with dve.Fori(0, NI) as it:
                dve.wait_ge(z["in"], 32 * (it + 1))
                statistics(lambda t: x0[:, t, :], mv, L0T, z["stats"], it * 3 * L0T)
                dve.wait_ge(z["rstd"], it + 1)
                dve.wait_ge(z["stored"], 16 * (it + 1))
                normalise(lambda t: xh0[:, t, :], lambda t: x0[:, t, :], mv, rstd, L0T, z["xhat"])
                dve.wait_ge(z["xT_hi"], it + 1)
                for kt in range(KT):
                    last = nc.vector.tensor_tensor(xTl[:, kt, :], xTf[:, kt, :], xTh[:, kt, :].bitcast(F32), ALU.subtract)
                last.then_inc(z["xT_split"], 1)
                dve.wait_ge(z["cT_hi"], it + 1)
                cps = bank[2][:, :].rearrange("p (k n) -> p k n", k=KT)[:, :, 0:L0B * SC]
                nc.vector.tensor_tensor(cTl[:, :, :], cps, cTh[:, :, :].bitcast(F32), ALU.subtract).then_inc(z["cT_split"], 1)
                dve.wait_ge(z["tokT_hi"], it + 1)
                tps = bank[3][:, :].rearrange("p (k n) -> p k n", k=KT)[:, :, 0:L0B * SC]
                for m in range(KT):
                    last = nc.vector.scalar_tensor_tensor(out=tTl[:, m, :], in0=tps[:, m, :],
                                                          scalar=pcol("L0_xattn_b_proj", m),
                                                          in1=tTh[:, m, :].bitcast(F32), op0=ALU.add, op1=ALU.subtract)
                last.then_inc(z["tokT_split"], 1)
                dve.wait_ge(z["tok"], it + 1)
                nc.vector.tensor_tensor(tkf[:, :, :], bank[4][0:SC, :].rearrange("p (b n) -> p b n", b=L0B),
                                        row("L0_xattn_b_proj")[0:SC].unsqueeze(1).broadcast_to([SC, L0B, D]),
                                        ALU.add).then_inc(z["tok_full"], 1)
                dve.wait_ge(z["psT"], it + 1)
                for kt in range(KT):
                    last = nc.vector.tensor_scalar(psf[:, kt, :], bank[6 + kt][:, :], pcol("L0_xattn_g_state", kt),
                                                   pcol("L0_xattn_beta_state", kt), ALU.mult, ALU.add)
                last.then_inc(z["ps_full"], 1)
                dve.wait_ge(z["scores"], it + 1)
                nc.vector.tensor_reduce(nm0[:, :], bank[5][:, :].rearrange("p (t n) -> p t n", t=L0T)[:, :, 0:SC],
                                        AX.X, ALU.max, negate=True).then_inc(z["negmax"], 1)
                dve.wait_ge(z["negmax"], 2 * it + 1)
                nc.vector.tensor_scalar(nms0[:, :], nm0[:, :], D ** -0.5, None, ALU.mult).then_inc(z["negmax"], 1)
                dve.wait_ge(z["tok_hi"], it + 1)
                nc.vector.tensor_tensor(tkl[:, :, :], tkf[:, :, :], tkh[:, :, :].bitcast(F32),
                                        ALU.subtract).then_inc(z["tok_split"], 1)
                dve.wait_ge(z["exp"], it + 1)
                nc.vector.reciprocal(rs0[:, :], sum0[:, :]).then_inc(z["rsum"], 1)
                dve.wait_ge(z["pT_hi"], it + 1)
                nc.vector.tensor_tensor(pTl0[:, :], bank[6][0:SC, :], pTh0[:, :].bitcast(F32),
                                        ALU.subtract).then_inc(z["pT_split"], 1)
                dve.wait_ge(z["ps_hi"], it + 1)
                nc.vector.tensor_tensor(psl[:, :, :], psf[:, :, :], psh[:, :, :].bitcast(F32),
                                        ALU.subtract).then_inc(z["ps_split"], 1)
                dve.wait_ge(z["rsum"], it + 1)
                dve.wait_ge(z["routed"], it + 1)
                for t in range(L0T):
                    nc.vector.tensor_scalar(rt[:, t, :], bank[(7 + t // 2) % 8][:, t % 2 * D:(t % 2 + 1) * D],
                                            rs0[:, t:t + 1], None, ALU.mult).then_inc(z["rt"], 1)
                dve.wait_ge(z["rt"], L0T * (it + 1))
                statistics(lambda t: rt[:, t, :], mv2, L0T, z["rstats"], it * 3 * L0T)
                dve.wait_ge(z["rrstd"], it + 1)
                normalise(lambda t: rt[:, t, :], lambda t: rt[:, t, :], mv2, rstd2, L0T, z["rhat"])
                dve.wait_ge(z["inT"], it + 1)
                for kt in range(KT):
                    last = nc.vector.tensor_scalar(inf[:, kt, :], bank[3 + kt][:, :], pcol("L0_xattn_g_input", kt),
                                                   pcol("L0_xattn_beta_input", kt), ALU.mult, ALU.add)
                last.then_inc(z["in_full"], 1)
                dve.wait_ge(z["in_hi"], it + 1)
                nc.vector.tensor_tensor(inl[:, :, :], inf[:, :, :], inh[:, :, :].bitcast(F32),
                                        ALU.subtract).then_inc(z["in_split"], 1)
                for m in range(KT):
                    dve.wait_ge(z["tanh_r"], it * KT + m + 1)
                    nc.vector.scalar_tensor_tensor(out=tr[:, m, :], in0=tr[:, m, :], scalar=1.0, in1=psf[:, m, :],
                                                   op0=ALU.add, op1=ALU.mult).then_inc(z["rps"], 1)
                for m in range(KT):
                    dve.wait_ge(z["rps_hi"], it * KT + m + 1)
                    nc.vector.scalar_tensor_tensor(out=rpl[:, m, :], in0=tr[:, m, :], scalar=0.5,
                                                   in1=rph[:, m, :].bitcast(F32), op0=ALU.mult,
                                                   op1=ALU.subtract).then_inc(z["rps_split"], 1)
                for m in range(KT):
                    dve.wait_ge(z["cand"], it * KT + m + 1)
                    nc.vector.tensor_tensor(cand[:, m, :], cand[:, m, :], xTf[:, m, :], ALU.subtract
                                            ).then_inc(z["new_step"], 1)
                for m in range(KT):
                    dve.wait_ge(z["tanh_u"], it * KT + m + 1)
                    dve.wait_ge(z["new_step"], it * 4 + m + 1)
                    nc.vector.scalar_tensor_tensor(out=cand[:, m, :], in0=tu[:, m, :], scalar=1.0, in1=cand[:, m, :],
                                                   op0=ALU.add, op1=ALU.mult).then_inc(z["new_step"], 1)
                for m in range(KT):
                    dve.wait_ge(z["new_step"], it * 4 + 3 + m)
                    nc.vector.scalar_tensor_tensor(out=cand[:, m, :], in0=cand[:, m, :], scalar=0.5, in1=xTf[:, m, :],
                                                   op0=ALU.mult, op1=ALU.add).then_inc(z["new"], 1)
                dve.wait_ge(z["new_tok"], it + 1)
                new_at = lambda t: bank[3 + t // 2][:, t % 2 * D:(t % 2 + 1) * D]
                statistics(new_at, mv, L0T, z["ostats"], it * 3 * L0T)
                dve.wait_ge(z["orstd"], it + 1)
                normalise(lambda t: xh0[:, t, :], new_at, mv, rstd, L0T, z["ohat"])
                dve.wait_ge(z["ohat"], it * (L0T + 1) + L0T)
                nc.vector.tensor_tensor(xh0[:, :, :], xh0[:, :, :],
                                        row("L0_xattn_g_out").unsqueeze(1).broadcast_to([128, L0T, D]),
                                        ALU.mult).then_inc(z["ohat"], 1)
                dve.wait_ge(z["ohat"], (it + 1) * (L0T + 1))
                nc.vector.tensor_tensor(xh0[:, :, :], xh0[:, :, :],
                                        row("L0_xattn_beta_out").unsqueeze(1).broadcast_to([128, L0T, D]),
                                        ALU.add).then_inc(z["out"], 1)

            def layernorm(a, it, gname, bname):
                dve.wait_ge(a["in"], 16 * (it + 1))
                statistics(lambda t: xin[:, t, :], mv, NT, a["stats"], it * 3 * NT)
                dve.wait_ge(a["rstd"], it + 1)
                normalise(lambda t: xhat[:, t, :], lambda t: xin[:, t, :], mv, rstd, NT, a["xhat"])
                dve.wait_ge(a["hT"], it + 1)
                for kt in range(KT):
                    nc.vector.tensor_scalar(hf[:, kt, :], bank[7][:, kt * S:(kt + 1) * S], pcol(gname, kt),
                                            pcol(bname, kt), ALU.mult, ALU.add).then_inc(a["h_full"], 1)
                dve.wait_ge(a["h_hi"], it + 1)
                nc.vector.tensor_tensor(hl[:, :, :], hf[:, :, :], hh[:, :, :].bitcast(F32),
                                        ALU.subtract).then_inc(a["h_split"], 1)

            def attention(a, it, cols):
                for s in range(PAIRS + 2):
                    if s < PAIRS:
                        g = s
                        dve.wait_ge(a["scores"], it * PAIRS + g + 1)
                        if cols == S:
                            for e in range(2):
                                nc.vector.tensor_reduce(negmax[:, g % 2, :, e],
                                                        bank[g % 2 * 2 + e][:, :].rearrange("p (t n) -> p t n", t=NT),
                                                        AX.X, ALU.max, negate=True).then_inc(a["negmax"], 1)
                        else:
                            nc.vector.tensor_reduce(
                                negmax[:, g % 2, :, :],
                                bank[g % 4][:, :].rearrange("p (t n) -> p t n", t=NT)[:, :, 0:2 * SC]
                                .rearrange("p t (e n) -> p t e n", e=2), AX.X, ALU.max, negate=True
                            ).then_inc(a["negmax"], 1)
                    if 1 <= s <= PAIRS:
                        g = s - 1
                        dve.wait_ge(a["exp"], it * HEADS + 2 * g + 2)
                        nc.vector.reciprocal(rs[:, g % 2, :, :], expsum[:, g % 2, :, :]).then_inc(a["rsum"], 1)
                        for e in range(2):
                            dve.wait_ge(a["pT_hi"], it * HEADS + 2 * g + e + 1)
                            r, n = (128, NT * S) if cols == S else (SC, S)
                            nc.vector.tensor_tensor(pTl[0:r, g % 2, e, 0:n], bank[4 + e][0:r, 0:n],
                                                    pTh[0:r, g % 2, e, 0:n].bitcast(F32),
                                                    ALU.subtract).then_inc(a["pT_lo"], 1)
                    if s >= 2:
                        g = s - 2
                        dve.wait_ge(a["rT_copied"], it * PAIRS + g + 1)
                        if g >= 1:
                            dve.wait_ge(a["o_lo"], it * PAIRS + g)
                        nc.vector.tensor_tensor(of[:, :], bank[6][:, 0:S], rT[:, :], ALU.mult).then_inc(a["o_norm"], 1)

            def residual(a, it, banks):
                dve.wait_ge(a["xb"], it + 1)
                dve.wait_ge(a["stored"], 16 * (it + 1))
                for t in range(NT):
                    last = nc.vector.tensor_tensor(xo[:, t, :], bank[banks[t]][:, 0:D], xb[:, t, :], ALU.add)
                last.then_inc(a["out"], 1)

            dve.wait_ge(z["out"], NI + 1)
            for a_, n_ in ((vh, 1), (vl, 2)):
                for pr in range(PAIRS):
                    last = nc.vector.memset(a_[:, :, pr * VW + DH:pr * VW + 2 * DH].bitcast(F32), 0.0)
            last.then_inc(zeros_ready, 1)
            weights_lo(dve, 1)
            with dve.Fori(0, B) as it:
                layernorm(a1, it, "L1_xattn_ln1_g", "L1_xattn_ln1_b")
                for g in range(PAIRS):
                    dve.wait_ge(a1["qk_hi"], it * PAIRS + g + 1)
                    nc.vector.tensor_tensor(qkl[:, g, :, :], bank[g % 4][:, :].rearrange("p (a n) -> p a n", a=2),
                                            qkh[:, g, :, :].bitcast(F32), ALU.subtract).then_inc(a1["qk_lo"], 1)
                for c in range(4):
                    dve.wait_ge(a1["v_hi"], it * 4 + c + 1)
                    nc.vector.tensor_tensor(v_dst(vl, 128, c), v_src(128, c), v_dst(vh, 128, c).bitcast(F32),
                                            ALU.subtract).then_inc(a1["v_lo"], 1)
                attention(a1, it, S)
                dve.wait_ge(a1["wo"], (it + 1) * PAIRS)
                residual(a1, it, (7, 0))
            dve.wait_ge(a1["out"], B + 1)
            for lo_ in (kdh, kdl):
                nc.vector.memset(lo_[0:DH, :, SC:2 * SC].bitcast(F32), 0.0)
                last = nc.vector.memset(lo_[DH:128, :, 0:SC].bitcast(F32), 0.0)
            last.then_inc(zeros_ready, 1)
            weights_lo(dve, 2)
            with dve.Fori(0, B) as it:
                dve.wait_ge(a2["cT_hi"], it + 1)
                nc.vector.tensor_tensor(cl[:, :, :], c_src(), ch[:, :, :].bitcast(F32), ALU.subtract).then_inc(a2["cT_lo"], 1)
                layernorm(a2, it, "L1_xattn_ln2_g", "L1_xattn_ln2_b")
                for c in range(2):
                    dve.wait_ge(a2["v_hi"], it * 2 + c + 1)
                    nc.vector.tensor_tensor(v_dst(vl, SC, c), v_src(SC, c), v_dst(vh, SC, c).bitcast(F32),
                                            ALU.subtract).then_inc(a2["v_lo"], 1)
                for c in range(2):
                    dve.wait_ge(a2["qk_hi"], it * 6 + c + 1)
                    for e in range(2):
                        last = nc.vector.tensor_tensor(k_dst(kdl, c, e), k_src(c, e), k_dst(kdh, c, e).bitcast(F32),
                                                       ALU.subtract)
                    last.then_inc(a2["qk_lo"], 1)
                for c in range(4):
                    dve.wait_ge(a2["qk_hi"], it * 6 + 3 + c)
                    nc.vector.tensor_tensor(qkl[:, 2 * c:2 * c + 2, 0, :], q_src(c),
                                            qkh[:, 2 * c:2 * c + 2, 0, :].bitcast(F32),
                                            ALU.subtract).then_inc(a2["qk_lo"], 1)
                attention(a2, it, SC)
                dve.wait_ge(a2["wo"], (it + 1) * PAIRS)
                residual(a2, it, (7, 0))
            dve.wait_ge(a2["out"], B + 1)
            weights_lo(dve, 3)
            with dve.Fori(0, B) as it:
                layernorm(f3, it, "L1_xattn_ln3_g", "L1_xattn_ln3_b")
                for j in range(FF // 128):
                    dve.wait_ge(f3["gelu"], it * 8 + j + 1)
                    if j >= 2:
                        dve.wait_ge(f3["f_lo"], it * 8 + j - 1)
                    nc.vector.scalar_tensor_tensor(out=fu[:, j % 2, :], in0=bank[j % 4][:, 0:S],
                                                   scalar=pp[:, NPC - 16 + j:NPC - 15 + j], in1=gl[:, j % 2, :],
                                                   op0=ALU.add, op1=ALU.mult).then_inc(f3["glu"], 1)
                    if j >= 1:
                        dve.wait_ge(f3["f_hi"], it * 8 + j)
                        nc.vector.tensor_tensor(fl[:, j - 1, :], fu[:, (j - 1) % 2, :], fh[:, j - 1, :].bitcast(F32),
                                                ALU.subtract).then_inc(f3["f_lo"], 1)
                dve.wait_ge(f3["f_hi"], it * 8 + 8)
                nc.vector.tensor_tensor(fl[:, 7, :], fu[:, 1, :], fh[:, 7, :].bitcast(F32),
                                        ALU.subtract).then_inc(f3["f_lo"], 1)
                dve.wait_ge(f3["down"], it + 1)
                residual(f3, it, (7, 6))

        @block.tensor
        def _(pe):
            def product(dst, terms):
                n = len(terms)
                for i, ((lh, ll), (rh, rl)) in enumerate(terms):
                    nc.tensor.matmul(dst, lh, rh, start=(i == 0), stop=False)
                    nc.tensor.matmul(dst, lh, rl, start=False, stop=False)
                    last = nc.tensor.matmul(dst, ll, rh, start=False, stop=(i == n - 1))
                return last

            pe.wait_ge(consts_in, 16 * (2 + len(ROWS)))
            pe.wait_ge(w_ready, WBASE[1])
            with pe.Fori(0, NI) as it:
                pe.wait_ge(z["in"], 32 * (it + 1))
                pe.wait_ge(z["out"], it + 1)
                for t in range(L0T):
                    for kt in range(KT):
                        last = nc.tensor.transpose(bank[kt][:, t * 128:(t + 1) * 128],
                                                   x0[:, t, kt * 128:(kt + 1) * 128], ident[:, :])
                last.then_inc(z["xT"], 1)
                for c in range(L0B):
                    for kt in range(KT):
                        last = nc.tensor.transpose(bank[2][:, kt * 256 + c * SC:kt * 256 + (c + 1) * SC],
                                                   c0[:, c, kt * 128:(kt + 1) * 128], ident[0:SC, 0:SC])
                last.then_inc(z["cT"], 1)
                pe.wait_ge(z["xhat"], L0T * (it + 1))
                for t in range(L0T):
                    for kt in range(KT):
                        last = nc.tensor.transpose(bank[6 + kt][:, t * 128:(t + 1) * 128],
                                                   xh0[:, t, kt * 128:(kt + 1) * 128], ident[:, :])
                last.then_inc(z["psT"], 1)
                pe.wait_ge(z["cT_split"], it + 1)
                for m in range(KT):
                    last = product(bank[3][:, m * 256:m * 256 + L0B * SC],
                                   [(wcols(0, "L0_xattn_W_proj", kt, m * 128, 128), (cTh[:, kt, :], cTl[:, kt, :]))
                                    for kt in range(KT)])
                last.then_inc(z["tokT"], 1)
                for c in range(L0B):
                    cc = slice(c * SC, (c + 1) * SC)
                    last = product(bank[4][0:SC, c * D:(c + 1) * D],
                                   [((cTh[:, kt, cc], cTl[:, kt, cc]), wcols(0, "L0_xattn_W_proj", kt, 0, D))
                                    for kt in range(KT)])
                last.then_inc(z["tok"], 1)
                pe.wait_ge(z["xT_split"], it + 1)
                pe.wait_ge(z["tokT_split"], it + 1)
                for t in range(L0T):
                    tt, cc = slice(t * 128, (t + 1) * 128), slice(t // NT * SC, (t // NT + 1) * SC)
                    last = product(bank[5][:, t * 128:t * 128 + SC],
                                   [((xTh[:, kt, tt], xTl[:, kt, tt]), (tTh[:, kt, cc], tTl[:, kt, cc]))
                                    for kt in range(KT)])
                last.then_inc(z["scores"], 1)
                pe.wait_ge(z["exp"], it + 1)
                pe.wait_ge(z["ps_full"], it + 1)
                for t in range(L0T):
                    last = nc.tensor.transpose(bank[6][0:SC, t * 128:(t + 1) * 128], p0[:, t, :], ident[:, :])
                last.then_inc(z["pT"], 1)
                pe.wait_ge(z["pT_split"], it + 1)
                pe.wait_ge(z["tok_split"], it + 1)
                for t in range(L0T):
                    tt = slice(t * 128, (t + 1) * 128)
                    last = product(bank[(7 + t // 2) % 8][:, t % 2 * D:(t % 2 + 1) * D],
                                   [((pTh0[:, tt], pTl0[:, tt]), (tkh[:, t // NT, :], tkl[:, t // NT, :]))])
                last.then_inc(z["routed"], 1)
                pe.wait_ge(z["rhat"], L0T * (it + 1))
                for t in range(L0T):
                    for kt in range(KT):
                        last = nc.tensor.transpose(bank[3 + kt][:, t * 128:(t + 1) * 128],
                                                   rt[:, t, kt * 128:(kt + 1) * 128], ident[:, :])
                last.then_inc(z["inT"], 1)
                pe.wait_ge(z["ps_split"], it + 1)
                pe.wait_ge(z["in_split"], it + 1)

                def gate(dst, name, m, state_h, state_l):
                    terms = [(wcols(0, name, 2 + kt, m * 128, 128), (inh[:, kt, :], inl[:, kt, :])) for kt in range(KT)]
                    terms += [(wcols(0, name, kt, m * 128, 128), (state_h[:, kt, :], state_l[:, kt, :]))
                              for kt in range(KT)]
                    return product(dst, terms)

                for m in range(KT):
                    gate(bank[5 + m][:, :], "L0_xattn_W_r", m, psh, psl).then_inc(z["gate_r"], 1)
                for m in range(KT):
                    gate(bank[(7 + m) % 8][:, :], "L0_xattn_W_u", m, psh, psl).then_inc(z["gate_u"], 1)
                pe.wait_ge(z["rps_split"], KT * (it + 1))
                for m in range(KT):
                    gate(bank[1 + m][:, :], "L0_xattn_W_n", m, rph, rpl).then_inc(z["gate_n"], 1)
                pe.wait_ge(z["new"], KT * (it + 1))
                for t in range(L0T):
                    for kt in range(KT):
                        last = nc.tensor.transpose(bank[3 + t // 2][:, t % 2 * D + kt * 128:t % 2 * D + (kt + 1) * 128],
                                                   cand[:, kt, t * 128:(t + 1) * 128], ident[:, :])
                last.then_inc(z["new_tok"], 1)

            def layernorm(a, it):
                pe.wait_ge(a["xhat"], NT * (it + 1))
                pe.wait_ge(a["out"], it + 1)
                for t in range(NT):
                    for kt in range(KT):
                        last = nc.tensor.transpose(bank[7][:, kt * S + t * 128:kt * S + (t + 1) * 128],
                                                   xhat[:, t, kt * 128:(kt + 1) * 128], ident[:, :])
                last.then_inc(a["hT"], 1)

            def scores(a, it, g, cols):
                if g >= 2:
                    pe.wait_ge(a["exp"], it * HEADS + 2 * (g - 1))
                if cols == S:
                    for t in range(NT):
                        tt = slice(t * 128, (t + 1) * 128)
                        for n, (lhs, rhs) in enumerate(((qkh, qkh), (qkh, qkl), (qkl, qkh))):
                            for e in range(2):
                                pr = slice(e * DH, (e + 1) * DH)
                                last = nc.tensor.matmul(bank[g % 2 * 2 + e][:, t * S:(t + 1) * S],
                                                        lhs[pr, g, 0, tt], rhs[pr, g, 1, :],
                                                        start=(n == 0), stop=(n == 2))
                else:
                    for t in range(NT):
                        tt = slice(t * 128, (t + 1) * 128)
                        last = product(bank[g % 4][:, t * S:t * S + 2 * SC],
                                       [((qkh[:, g, 0, tt], qkl[:, g, 0, tt]), (kdh[:, g, :], kdl[:, g, :]))])
                last.then_inc(a["scores"], 1)

            def transpose_p(a, it, g, cols):
                for e in range(2):
                    pe.wait_ge(a["exp"], it * HEADS + 2 * g + e + 1)
                    if g >= 1:
                        pe.wait_ge(a["pT_lo"], it * HEADS + 2 * g + e - 1)
                    for t in range(NT):
                        for j in range(NT if cols == S else 1):
                            n = min(cols, 128)
                            last = nc.tensor.transpose(bank[4 + e][0:n, j * S + t * 128:j * S + (t + 1) * 128],
                                                       p[:, g % 2, e, t * cols + j * 128:t * cols + j * 128 + n],
                                                       ident[:, :])
                    last.then_inc(a["pT"], 1)

            def weighted_values(a, it, g, cols):
                r = min(cols, 128)
                pe.wait_ge(a["rsum_wide"], it * PAIRS + g + 1)
                if g >= 1:
                    pe.wait_ge(a["o_norm"], it * PAIRS + g)
                for t in range(NT):
                    nc.tensor.transpose(bank[6][:, S + t * 128:S + (t + 1) * 128],
                                        rsb[:, g % 2, t, :], ident[:, :])
                terms = []
                for e in range(2):
                    for j in range(NT if cols == S else 1):
                        vc = slice(g * VW + e * DH, g * VW + e * DH + 128)
                        pc = slice(j * S, (j + 1) * S)
                        terms.append(((vh[0:r, j, vc], vl[0:r, j, vc]), (pTh[0:r, g % 2, e, pc], pTl[0:r, g % 2, e, pc])))
                pe.wait_ge(a["pT_lo"], it * HEADS + 2 * g + 2)
                product(bank[6][:, 0:S], terms).then_inc(a["o"], 1)

            def attention(a, it, cols, phase, wo):
                scores(a, it, 0, cols)
                for s in range(PAIRS + 1):
                    if s + 1 < PAIRS:
                        scores(a, it, s + 1, cols)
                    if s < PAIRS:
                        transpose_p(a, it, s, cols)
                    if s >= 1:
                        weighted_values(a, it, s - 1, cols)
                for g in range(PAIRS):
                    pe.wait_ge(a["o_lo"], it * PAIRS + g + 1)
                    for t in range(NT):
                        tt = slice(t * 128, (t + 1) * 128)
                        wh, wl = wcols(phase, wo, g, 0, D)
                        dst = bank[7 - 7 * t][:, 0:D]
                        nc.tensor.matmul(dst, oh[:, g, tt], wh, start=(g == 0), stop=False)
                        nc.tensor.matmul(dst, oh[:, g, tt], wl, start=False, stop=False)
                        last = nc.tensor.matmul(dst, ol[:, g, tt], wh, start=False, stop=(g == PAIRS - 1))
                    last.then_inc(a["wo"], 1)

            pe.wait_ge(w_ready, WBASE[2])
            pe.wait_ge(zeros_ready, 1)
            with pe.Fori(0, B) as it:
                layernorm(a1, it)
                pe.wait_ge(a1["h_split"], it + 1)
                h = [(hh[:, kt, :], hl[:, kt, :]) for kt in range(KT)]
                for g in range(PAIRS):
                    if g >= 4:
                        pe.wait_ge(a1["qk_lo"], it * PAIRS + g - 3)
                    for i, w in enumerate(("L1_xattn_a1_Wq", "L1_xattn_a1_Wk")):
                        last = product(bank[g % 4][:, i * S:(i + 1) * S],
                                       [(wcols(1, w, kt, g * 128, 128), h[kt]) for kt in range(KT)])
                    last.then_inc(a1["qk"], 1)
                for c in range(4):
                    tt = slice(c // 2 * 128, (c // 2 + 1) * 128)
                    product(bank[4 + c][:, :],
                            [((hh[:, kt, tt], hl[:, kt, tt]), wcols(1, "L1_xattn_a1_Wv", kt, c % 2 * 512, 512))
                             for kt in range(KT)]).then_inc(a1["v"], 1)
                pe.wait_ge(a1["qk_lo"], (it + 1) * PAIRS)
                pe.wait_ge(a1["v_lo"], (it + 1) * 4)
                attention(a1, it, S, 1, "L1_xattn_a1_Wo")

            pe.wait_ge(w_ready, WBASE[3])
            pe.wait_ge(zeros_ready, 2)
            with pe.Fori(0, B) as it:
                pe.wait_ge(a2["c_in"], 16 * (it + 1))
                pe.wait_ge(a2["out"], it + 1)
                for kt in range(KT):
                    last = nc.tensor.transpose(bank[6][:, kt * 256:kt * 256 + SC], cin[:, kt * 128:(kt + 1) * 128],
                                               ident[0:SC, 0:SC])
                last.then_inc(a2["cT"], 1)
                layernorm(a2, it)
                pe.wait_ge(a2["cT_lo"], it + 1)
                cT = [(ch[:, kt, :], cl[:, kt, :]) for kt in range(KT)]
                for c in range(2):
                    product(bank[c][0:SC, :], [(cT[kt], wcols(2, "L1_xattn_a2_Wv", kt, c * 512, 512))
                                               for kt in range(KT)]).then_inc(a2["v"], 1)
                for c in range(2):
                    for g in range(4):
                        last = product(bank[2 + c][:, g * SC:(g + 1) * SC],
                                       [(wcols(2, "L1_xattn_a2_Wk", kt, (4 * c + g) * 128, 128), cT[kt])
                                        for kt in range(KT)])
                    last.then_inc(a2["qk"], 1)
                pe.wait_ge(a2["h_split"], it + 1)
                for c in range(4):
                    for g in range(2):
                        last = product(bank[4 + c][:, g * S:(g + 1) * S],
                                       [(wcols(2, "L1_xattn_a2_Wq", kt, (2 * c + g) * 128, 128),
                                         (hh[:, kt, :], hl[:, kt, :])) for kt in range(KT)])
                    last.then_inc(a2["qk"], 1)
                pe.wait_ge(a2["v_lo"], (it + 1) * 2)
                pe.wait_ge(a2["qk_lo"], (it + 1) * 6)
                attention(a2, it, SC, 2, "L1_xattn_a2_Wo")

            pe.wait_ge(w_ready, WBASE[4])
            with pe.Fori(0, B) as it:
                layernorm(f3, it)
                pe.wait_ge(f3["h_split"], it + 1)
                for j in range(FF // 128):
                    if j >= 4:
                        pe.wait_ge(f3["glu"], it * 8 + j - 3)
                    for i in range(2):
                        last = product(bank[j % 4][:, i * S:(i + 1) * S],
                                       [(wcols(3, "L1_xattn_ff_Wp", kt, i * FF + j * 128, 128),
                                         (hh[:, kt, :], hl[:, kt, :])) for kt in range(KT)])
                    last.then_inc(f3["up"], 1)
                for j in range(FF // 128):
                    pe.wait_ge(f3["f_lo"], it * 8 + j + 1)
                    for t in range(NT):
                        tt = slice(t * 128, (t + 1) * 128)
                        wh, wl = wcols(3, "L1_xattn_ff_Wo", j, 0, D)
                        dst = bank[7 - t][:, 0:D]
                        nc.tensor.matmul(dst, fh[:, j, tt], wh, start=(j == 0), stop=False)
                        nc.tensor.matmul(dst, fh[:, j, tt], wl, start=False, stop=False)
                        last = nc.tensor.matmul(dst, fl[:, j, tt], wh, start=False, stop=(j == 7))
                last.then_inc(f3["down"], 1)


def kernel(**inputs):
    import numpy as _np
    import concourse.bacc as _bacc
    from concourse import mybir as _mybir
    from concourse.bass_utils import run_bass_kernel_spmd as _run

    a = {k: _np.asarray(v) for k, v in inputs.items()}
    f32 = _np.float32

    def tiles(w):
        k, n = w.shape
        kt = -(-k // 128)
        padded = _np.zeros((kt * 128, n), f32)
        padded[:k] = w
        return padded.reshape(kt, 128, n).transpose(1, 0, 2).reshape(128, kt * n)

    chunks = []
    for ws, n in zip(WSETS, WCHUNKS):
        packed = _np.zeros((128, n * CH), f32)
        at = 0
        for w in ws:
            packed[:, at:at + WIDTH[w]] = tiles(a[w])
            at += WIDTH[w]
        chunks.append(packed.reshape(128, n, CH).transpose(1, 0, 2))
    ctx_padded = _np.zeros((B, SC, D), f32)
    ctx_padded[:, :, :DC] = a["ctx_768"]
    vectors = _np.concatenate([a[n] for n in PCOLS] + [a["L1_xattn_ff_bp"]])
    arrays = {
        "in_x": _np.ascontiguousarray(a["x"]),
        "in_ctx": ctx_padded,
        "in_weights": _np.ascontiguousarray(_np.concatenate(chunks)),
        "in_params": _np.ascontiguousarray(vectors.reshape(NPC, 128).T),
        "in_rows": _np.stack([a[n] for n in ROWS]),
        "in_ident": _np.eye(128, dtype=f32),
    }
    nc = _bacc.Bacc("TRN2", target_bir_lowering=False, num_devices=1)
    aps = [nc.dram_tensor(n, v.shape, _mybir.dt.float32, kind="ExternalInput").ap() for n, v in arrays.items()]
    mid = [nc.dram_tensor(f"x{i}_dram", (B, S, D), _mybir.dt.float32, kind="Internal").ap() for i in (1, 2, 3)]
    out = nc.dram_tensor("out_0_dram", (B, S, D), _mybir.dt.float32, kind="ExternalOutput").ap()
    build(nc, *aps, *mid, out)
    return _run(nc, [arrays], core_ids=[0]).results[0]["out_0_dram"]
```

```python
from collections import namedtuple
from contextlib import ExitStack

import concourse.bass as bass
from concourse import mybir

F32 = mybir.dt.float32
F32R = mybir.dt.float32r
ALU = mybir.AluOpType
ACT = mybir.ActivationFunctionType
AX = mybir.AxisListType

B, S, D = 8, 256, 256
SC, DC = 120, 192
HEADS, DH = 16, 64
PAIRS = HEADS // 2
FF = 1024
KT = D // 128
NT = S // 128
EPS = 1e-5
L0B = 2
L0T = L0B * NT
CH = 1024
STAGES = 4
VW = 3 * DH

PCOLS = ["L0_xattn_g_state", "L0_xattn_beta_state", "L0_xattn_g_input", "L0_xattn_beta_input",
         "L0_xattn_b_u", "L0_xattn_b_r", "L0_xattn_b_n", "L0_xattn_b_proj",
         "L1_xattn_ln1_g", "L1_xattn_ln1_b", "L1_xattn_ln2_g", "L1_xattn_ln2_b",
         "L1_xattn_ln3_g", "L1_xattn_ln3_b"]
NPC = KT * len(PCOLS) + 2 * FF // 128
ROWS = ["L0_xattn_b_proj", "L0_xattn_g_out", "L0_xattn_beta_out", "L1_xattn_a1_bo", "L1_xattn_a2_bo", "L1_xattn_ff_bo"]
WSETS = [["L0_xattn_W_proj", "L0_xattn_W_r", "L0_xattn_W_u", "L0_xattn_W_n"],
         ["L1_xattn_a1_Wq", "L1_xattn_a1_Wk", "L1_xattn_a1_Wv", "L1_xattn_a1_Wo"],
         ["L1_xattn_a2_Wq", "L1_xattn_a2_Wk", "L1_xattn_a2_Wv", "L1_xattn_a2_Wo"],
         ["L1_xattn_ff_Wp", "L1_xattn_ff_Wo"]]
KTILES = {"L0_xattn_W_proj": 2, "L0_xattn_W_r": 4, "L0_xattn_W_u": 4, "L0_xattn_W_n": 4,
          "L1_xattn_a1_Wq": 2, "L1_xattn_a1_Wk": 2, "L1_xattn_a1_Wv": 2, "L1_xattn_a1_Wo": PAIRS,
          "L1_xattn_a2_Wq": 2, "L1_xattn_a2_Wk": 2, "L1_xattn_a2_Wv": 2, "L1_xattn_a2_Wo": PAIRS,
          "L1_xattn_ff_Wp": 2, "L1_xattn_ff_Wo": FF // 128}
NCOL = {w: D if w.startswith("L0") or w.endswith("Wo") else 2 * FF if w.endswith("Wp") else HEADS * DH for w in KTILES}
WIDTH = {w: KTILES[w] * NCOL[w] for w in KTILES}
WCHUNKS = [-(-sum(WIDTH[w] for w in ws) // CH) for ws in WSETS]
QCHUNKS = KT * HEADS * DH // CH


SPLITS = [(0, c) for c in range(4)] + [(1, c) for c in (4, 5, 6, 7, 0, 1, 2, 3)] + [(2, c) for c in range(8)] \
    + [(3, c) for c in range(6)]
EARLY = 8
AT_A1, AT_A2, AT_A2_WO, AT_FF = 12, 18, 20, 26
CHUNK_AT = [sum(WCHUNKS[:ph]) + c for ph, c in SPLITS]

Phase = namedtuple("Phase", "n sem cols gamma beta bias wo")


def build(nc, x, ctx_p, weights, params, rows, ident_in, x1_dram, x2_dram, x3_dram, out):
    es = ExitStack()
    with es:
        def sb(name, shape, dt=F32, where=es):
            return where.enter_context(nc.sbuf_tensor(name, shape, dt))

        def sem(name):
            return es.enter_context(nc.semaphore(name))

        WH = sb("w_hi", [128, 8 * CH], F32R)
        WL = sb("w_lo", [128, 8 * CH], F32R)
        stage = sb("w_stage", [128, STAGES, CH])
        pp = sb("params_pp", [128, NPC])
        rb = sb("rows_bc", [128, len(ROWS), D])
        ident = sb("ident", [128, 128])
        neg_half = sb("neg_half", [128, L0T])
        ones = sb("ones", [128, S])
        half_b = sb("half_b", [128, 2 * KT])
        mv = sb("mean_var", [128, L0T, 2])
        mv2 = sb("mean_var2", [128, L0T, 2])
        st6 = sb("bn6", [128, L0T, 6])
        rstd = sb("rstd", [128, L0T])
        rstd2 = sb("rstd2", [128, L0T])

        def pcol(name, kt):
            i = KT * PCOLS.index(name) + kt
            return pp[:, i:i + 1]

        def row(name):
            return rb[:, ROWS.index(name), :]

        with ExitStack() as l0:
            x0 = sb("l0_x", [128, L0T, D], where=l0)
            c0 = sb("l0_ctx", [SC, L0B, D], where=l0)
            xTf = sb("l0_xT", [128, KT, L0T * 128], where=l0)
            xTh = sb("l0_xT_hi", [128, KT, L0T * 128], F32R, where=l0)
            xTl = sb("l0_xT_lo", [128, KT, L0T * 128], F32R, where=l0)
            cTh = sb("l0_cT_hi", [128, KT, L0B * SC], F32R, where=l0)
            cTl = sb("l0_cT_lo", [128, KT, L0B * SC], F32R, where=l0)
            tTh = sb("l0_tokT_hi", [128, KT, L0B * SC], F32R, where=l0)
            tTl = sb("l0_tokT_lo", [128, KT, L0B * SC], F32R, where=l0)
            tkf = sb("l0_tok", [SC, L0B, D], where=l0)
            tkh = sb("l0_tok_hi", [SC, L0B, D], F32R, where=l0)
            tkl = sb("l0_tok_lo", [SC, L0B, D], F32R, where=l0)
            nm0 = sb("l0_negmax", [128, L0T], where=l0)
            nms0 = sb("l0_negmax_scaled", [128, L0T], where=l0)
            sum0 = sb("l0_sum", [128, L0T], where=l0)
            rs0 = sb("l0_rsum", [128, L0T], where=l0)
            p0 = sb("l0_p", [128, L0T, SC], where=l0)
            pTh0 = sb("l0_pT_hi", [SC, L0T * 128], F32R, where=l0)
            pTl0 = sb("l0_pT_lo", [SC, L0T * 128], F32R, where=l0)
            rt = sb("l0_routed", [128, L0T, D], where=l0)
            xh0 = sb("l0_xhat", [128, L0T, D], where=l0)
            psf = sb("l0_psT", [128, KT, L0T * 128], where=l0)
            psh = sb("l0_psT_hi", [128, KT, L0T * 128], F32R, where=l0)
            psl = sb("l0_psT_lo", [128, KT, L0T * 128], F32R, where=l0)
            inf = sb("l0_inT", [128, KT, L0T * 128], where=l0)
            inh = sb("l0_inT_hi", [128, KT, L0T * 128], F32R, where=l0)
            inl = sb("l0_inT_lo", [128, KT, L0T * 128], F32R, where=l0)
            tr = sb("l0_tanh_r", [128, KT, L0T * 128], where=l0)
            rph = sb("l0_rps_hi", [128, KT, L0T * 128], F32R, where=l0)
            rpl = sb("l0_rps_lo", [128, KT, L0T * 128], F32R, where=l0)
            tu = sb("l0_tanh_u", [128, KT, L0T * 128], where=l0)
            x1o = sb("l0_out", [128, L0T, D], where=l0)
            cand = sb("l0_cand", [128, KT, L0T * 128], where=l0)

        with ExitStack() as l1:
            xin = sb("x_in", [128, NT, D], where=l1)
            xhat = sb("xhat", [128, NT, D], where=l1)
            xb = sb("x_plus_bias", [128, NT, D], where=l1)
            hf = sb("hT", [128, KT, S], where=l1)
            hh = sb("hT_hi", [128, KT, S], F32R, where=l1)
            hl = sb("hT_lo", [128, KT, S], F32R, where=l1)
            xo = sb("x_out", [128, NT, D], where=l1)
            with ExitStack() as att:
                qkh = sb("qkT_hi", [128, PAIRS, 2, S], F32R, where=att)
                qkl = sb("qkT_lo", [128, PAIRS, 2, S], F32R, where=att)
                vh = sb("v_hi", [128, NT, PAIRS * VW], F32R, where=att)
                vl = sb("v_lo", [128, NT, PAIRS * VW], F32R, where=att)
                p = sb("p", [128, 2, 2, NT * S], where=att)
                pTh = sb("pT_hi", [128, 2, 2, NT * S], F32R, where=att)
                pTl = sb("pT_lo", [128, 2, 2, NT * S], F32R, where=att)
                negmax = sb("negmax", [128, 2, NT, 2], where=att)
                expsum = sb("expsum", [128, 2, NT, 2], where=att)
                rs = sb("rsum", [128, 2, NT * 2], where=att)
                rsw = sb("rsum_wide", [128, 2, NT, 2 * DH], where=att)
                rT = sb("rsumT", [128, S], where=att)
                of = sb("oT", [128, S], where=att)
                oh = sb("oT_hi", [128, PAIRS, S], F32R, where=att)
                ol = sb("oT_lo", [128, PAIRS, S], F32R, where=att)
                cin = sb("ctx_in", [SC, D], where=att)
                ch = sb("cT_hi", [128, KT, SC], F32R, where=att)
                cl = sb("cT_lo", [128, KT, SC], F32R, where=att)
            kdh = qkh[:, :, 1, 0:2 * SC]
            kdl = qkl[:, :, 1, 0:2 * SC]
            gl = p[:, 0, 0, :].rearrange("p (a n) -> p a n", a=2)
            fu = p[:, 0, 1, :].rearrange("p (a n) -> p a n", a=2)
            fh = qkh[:, :, 0, :]
            fl = qkl[:, :, 0, :]

        bank = [es.enter_context(nc.psum_tensor(f"bank{i}", [128, 512], F32)) for i in range(8)]

        consts_in = sem("consts_in")
        passed = sem("passed")
        neg_half_ready = sem("neg_half_ready")
        half_b_ready = sem("half_b_ready")
        zeros_ready = sem("zeros_ready")
        staged = [sem(f"weights_staged{i}") for i in range(STAGES)]
        w_hi_ready = sem("w_hi_ready")
        w_ready = sem("w_ready")
        z = {n: sem("l0_" + n) for n in (
            "in", "xT", "cT", "xT_full", "xT_hi", "xT_split", "cT_hi", "cT_split", "stats", "rstd", "xhat",
            "tokT", "tok", "tokT_hi", "tokT_split", "tok_full", "tok_hi", "tok_split", "scores", "negmax", "exp",
            "rsum", "pT", "pT_hi", "pT_split", "routed", "rt", "rstats", "rrstd", "rhat", "psT", "ps_full", "ps_hi",
            "ps_split", "inT", "in_full", "in_hi", "in_split", "gate_r", "tanh_r", "rps", "rps_hi", "rps_split",
            "gate_u", "tanh_u", "gate_n", "cand", "new", "new_step", "new_tok", "ostats", "orstd", "ohat", "out",
            "stored")}

        def phase_sems(tag, names):
            return {n: sem(f"{tag}_{n}") for n in names}

        LN = ("in", "xb", "stats", "rstd", "xhat", "hT", "h_full", "h_hi", "h_split", "out", "stored")
        AT = LN + ("qk", "qk_hi", "qk_lo", "v", "v_hi", "v_lo", "scores", "negmax", "exp", "rsum", "pT", "pT_hi",
                   "pT_lo", "rT", "rT_copied", "o", "o_norm", "o_hi", "o_lo", "wo", "c_in", "cT", "cT_hi", "cT_lo")
        a1 = phase_sems("a1", AT)
        a2 = phase_sems("a2", AT)
        f3 = phase_sems("ff", LN + ("up", "gelu", "glu", "f_hi", "f_lo", "down"))
        NI = B // L0B
        A1 = Phase(1, a1, S, "L1_xattn_ln1_g", "L1_xattn_ln1_b", "L1_xattn_a1_bo", "L1_xattn_a1_Wo")
        A2 = Phase(2, a2, SC, "L1_xattn_ln2_g", "L1_xattn_ln2_b", "L1_xattn_a2_bo", "L1_xattn_a2_Wo")
        FFN = Phase(3, f3, 0, "L1_xattn_ln3_g", "L1_xattn_ln3_b", "L1_xattn_ff_bo", "L1_xattn_ff_Wo")

        def wcols(phase, name, kt, lo_col, n):
            base = 0
            for w in WSETS[phase]:
                if w == name:
                    break
                base += WIDTH[w]
            a = base + kt * NCOL[name] + lo_col
            return WH[:, a:a + n], WL[:, a:a + n]

        def load_weights(sp, first, last):
            for n in range(first, last):
                if n >= STAGES:
                    sp.wait_ge(w_ready, n - STAGES + 1)
                sp.dma_start(stage[:, n % STAGES, :], weights[CHUNK_AT[n]]).then_inc(staged[n % STAGES], 16)

        def weights_hi(act, n):
            phase, c = SPLITS[n]
            act.wait_ge(staged[n % STAGES], 16 * (n // STAGES + 1))
            src, dst = stage[:, n % STAGES, :], WH[:, c * CH:(c + 1) * CH]
            if phase in (1, 2) and c < QCHUNKS:
                nc.scalar.mul(dst, src, DH ** -0.5).then_inc(w_hi_ready, 1)
            else:
                nc.scalar.copy(dst, src).then_inc(w_hi_ready, 1)

        def weights_lo(dve, n):
            phase, c = SPLITS[n]
            dve.wait_ge(staged[n % STAGES], 16 * (n // STAGES + 1))
            dve.wait_ge(w_hi_ready, n + 1)
            src, dst = stage[:, n % STAGES, :], WL[:, c * CH:(c + 1) * CH]
            hi = WH[:, c * CH:(c + 1) * CH].bitcast(F32)
            if phase in (1, 2) and c < QCHUNKS:
                nc.vector.scalar_tensor_tensor(out=dst, in0=src, scalar=DH ** -0.5, in1=hi,
                                               op0=ALU.mult, op1=ALU.subtract).then_inc(w_ready, 1)
            else:
                nc.vector.tensor_tensor(dst, src, hi, ALU.subtract).then_inc(w_ready, 1)

        def v_src(r, c):
            return bank[(4, 5, 2, 3)[c]][0:r, :].rearrange("p (g e d) -> p g e d", g=4, e=2)

        def v_dst(buf, r, c):
            half = slice(c % 2 * 4 * VW, (c % 2 + 1) * 4 * VW)
            return buf[0:r, c // 2, half].rearrange("p (g s d) -> p g s d", g=4, s=3)[:, :, 0:3:2, :]

        def first_c():
            return bank[2][:, :].rearrange("p (k n) -> p k n", k=KT)[:, :, 0:L0B * SC]

        def first_tokT():
            return bank[4][:, :].rearrange("p (k n) -> p k n", k=KT)[:, :, 0:L0B * SC]

        def c_src():
            return bank[7][:, :].rearrange("p (k n) -> p k n", k=KT)[:, :, 0:SC]

        def k_src(c, e):
            return bank[2 + c][e * DH:(e + 1) * DH, 0:4 * SC].rearrange("p (g n) -> p g n", g=4)

        def k_dst(buf, c, e):
            return buf[e * DH:(e + 1) * DH, 4 * c:4 * c + 4, e * SC:(e + 1) * SC]

        def q_src(c):
            return bank[(0, 1, 4, 5)[c]][:, :].rearrange("p (g n) -> p g n", g=2)

        def scores_at(cols, g, e, t):
            if cols == S:
                return bank[g % 2 * 2 + e][:, t * S:(t + 1) * S]
            return bank[g % 4][:, t * S + e * SC:t * S + (e + 1) * SC]

        def apart(engine):
            engine.sem_inc(passed, 1)

        block = es.enter_context(nc.Block())

        @block.sync
        def _(sp):
            for a in (z, a1, a2, f3):
                sp.sem_inc(a["stored"], 16)
            sp.dma_start(pp[:, :], params).then_inc(consts_in, 16)
            sp.dma_start(ident[:, :], ident_in).then_inc(consts_in, 16)
            for i in range(len(ROWS)):
                sp.dma_start(rb[:, i, :], rows[i:i + 1, :].partition_broadcast(128)).then_inc(consts_in, 16)
            def batches(dram, first, n):
                return dram[bass.ds(first, n), :, :].rearrange("b (t p) d -> p (b t) d", p=128)

            def load_first(it):
                sp.dma_start(x0[:, :, :], batches(x, it * L0B, L0B)).then_inc(z["in"], 16)
                csrc = ctx_p[bass.ds(it * L0B, L0B), :, :].rearrange("b s d -> s b d")
                sp.dma_start(c0[:, :, :], csrc).then_inc(z["in"], 16)

            def store_first(it):
                sp.wait_ge(z["out"], it + 1)
                apart(sp)
                sp.dma_start(batches(x1_dram, it * L0B, L0B), x1o[:, :, :]).then_inc(z["stored"], 16)

            def next_first(it):
                sp.wait_ge(z["xT"], it + 1)
                apart(sp)
                sp.wait_ge(z["cT"], it + 1)
                apart(sp)
                sp.wait_ge(z["xhat"], (it + 1) * L0T)
                apart(sp)
                load_first(it + 1)

            load_first(0)
            load_weights(sp, 0, AT_A1)
            next_first(0)
            with sp.Fori(0, NI - 2) as i:
                next_first(i + 1)
                store_first(i)
            store_first(NI - 2)
            store_first(NI - 1)
            sp.wait_ge(z["stored"], 16 * (NI + 1))

            source = {1: x1_dram, 2: x2_dram, 3: x3_dram}
            result = {1: x2_dram, 2: x3_dram, 3: out}

            def load(ph, it):
                sp.dma_start(xin[:, :, :], batches(source[ph.n], it, 1)).then_inc(ph.sem["in"], 16)
                if ph.n == 2:
                    sp.dma_start(cin[:, :], ctx_p[bass.ds(it, 1), :, :].rearrange("b s d -> (b s) d")
                                 ).then_inc(ph.sem["c_in"], 16)

            def store(ph, it):
                sp.wait_ge(ph.sem["out"], it + 1)
                apart(sp)
                sp.dma_start(batches(result[ph.n], it, 1), xo[:, :, :]).then_inc(ph.sem["stored"], 16)

            def iteration(ph, it, prev, nxt):
                if prev:
                    store(*prev)
                    if prev[0] is not ph:
                        sp.wait_ge(prev[0].sem["stored"], 16 * (B + 1))
                if nxt:
                    sp.wait_ge(ph.sem["xb"], it + 1)
                    apart(sp)
                    sp.wait_ge(ph.sem["xhat"], (it + 1) * NT)
                    apart(sp)
                    if ph is A2:
                        sp.wait_ge(a2["cT"], it + 1)
                        apart(sp)
                    if nxt[0] is not ph:
                        sp.wait_ge(ph.sem["stored"], 16 * B)
                    load(*nxt)
                if ph is FFN:
                    store(ph, it)

            load(A1, 0)
            load_weights(sp, AT_A1, AT_A1 + STAGES)
            iteration(A1, 0, None, (A1, 1))
            with sp.Fori(0, B - 2) as i:
                iteration(A1, i + 1, (A1, i), (A1, i + 2))
            iteration(A1, B - 1, (A1, B - 2), (A2, 0))
            load_weights(sp, AT_A1 + STAGES, AT_A2 + STAGES)
            iteration(A2, 0, (A1, B - 1), (A2, 1))
            load_weights(sp, AT_A2 + STAGES, AT_A2_WO + STAGES)
            with sp.Fori(0, B - 2) as i:
                iteration(A2, i + 1, (A2, i), (A2, i + 2))
            iteration(A2, B - 1, (A2, B - 2), (FFN, 0))
            load_weights(sp, AT_A2_WO + STAGES, AT_FF)
            iteration(FFN, 0, (A2, B - 1), (FFN, 1))
            with sp.Fori(0, B - 2) as i:
                iteration(FFN, i + 1, None, (FFN, i + 2))
            iteration(FFN, B - 1, None, None)
            sp.wait_ge(f3["stored"], 16 * (B + 1))

        @block.gpsimd
        def _(pool):
            nc.gpsimd.memset(neg_half[:, :], -0.5).then_inc(neg_half_ready, 1)
            pool.wait_ge(neg_half_ready, 1)

            def inverse_std(dst, src, n, waited, count, done):
                pool.wait_ge(waited, count)
                nc.gpsimd.tensor_tensor(dst[:, 0:n], src[:, 0:n, 1], neg_half[:, 0:n], ALU.pow).then_inc(done, 1)

            def full_xT(it, last_used):
                pool.wait_ge(z["xT_split"], it + 1)
                if last_used is not None:
                    pool.wait_ge(z["new"], last_used)
                nc.gpsimd.tensor_tensor(xTf[:, :, :], xTh[:, :, :].bitcast(F32), xTl[:, :, :].bitcast(F32),
                                        ALU.add).then_inc(z["xT_full"], 1)

            def first_layer(it, front):
                if front:
                    inverse_std(rstd, mv, L0T, z["stats"], (it + 2) * 3 * L0T, z["rstd"])
                    inverse_std(rstd2, mv2, L0T, z["rstats"], (it + 2) * 3 * L0T, z["rrstd"])
                inverse_std(rstd, mv, L0T, z["ostats"], (it + 1) * 3 * L0T, z["orstd"])
                if front:
                    full_xT(it + 1, (it + 1) * KT)

            inverse_std(rstd, mv, L0T, z["stats"], 3 * L0T, z["rstd"])
            full_xT(0, None)
            inverse_std(rstd2, mv2, L0T, z["rstats"], 3 * L0T, z["rrstd"])
            first_layer(0, True)
            with pool.Fori(0, NI - 2) as i:
                first_layer(i + 1, True)
            first_layer(NI - 1, False)
            nc.gpsimd.memset(ones[:, :], 1.0).then_inc(neg_half_ready, 1)
            pool.wait_ge(neg_half_ready, 2)

            def add_bias(ph, it, prev):
                pool.wait_ge(ph.sem["in"], (it + 1) * 16)
                if prev:
                    pool.wait_ge(prev[0].sem["out"], prev[1] + 1)
                nc.gpsimd.tensor_tensor(xb[:, :, :], xin[:, :, :],
                                        row(ph.bias).unsqueeze(1).broadcast_to([128, NT, D]),
                                        ALU.add).then_inc(ph.sem["xb"], 1)

            def prepare(ph, it):
                inverse_std(rstd, mv, NT, ph.sem["stats"], (it + 1) * 3 * NT, ph.sem["rstd"])

            def attention(ph, it, prev, nxt):
                a = ph.sem
                add_bias(ph, it, prev)
                for g in range(PAIRS):
                    if g == 2:
                        prepare(*nxt)
                    pool.wait_ge(a["o_norm"], it * PAIRS + g + 1)
                    nc.gpsimd.tensor_tensor(oh[:, g, :], of[:, :], ones[:, :], ALU.mult).then_inc(a["o_hi"], 1)
                    pool.wait_ge(a["o_hi"], it * PAIRS + g + 1)
                    nc.gpsimd.tensor_tensor(ol[:, g, :], of[:, :], oh[:, g, :].bitcast(F32),
                                            ALU.subtract).then_inc(a["o_lo"], 1)

            def feed_forward(it, prev, nxt):
                add_bias(FFN, it, prev)
                if nxt:
                    prepare(*nxt)

            prepare(A1, 0)
            attention(A1, 0, None, (A1, 1))
            with pool.Fori(0, B - 2) as i:
                attention(A1, i + 1, (A1, i), (A1, i + 2))
            attention(A1, B - 1, (A1, B - 2), (A2, 0))
            attention(A2, 0, (A1, B - 1), (A2, 1))
            with pool.Fori(0, B - 2) as i:
                attention(A2, i + 1, (A2, i), (A2, i + 2))
            attention(A2, B - 1, (A2, B - 2), (FFN, 0))
            feed_forward(0, (A2, B - 1), (FFN, 1))
            with pool.Fori(0, B - 2) as i:
                feed_forward(i + 1, (FFN, i), (FFN, i + 2))
            feed_forward(B - 1, (FFN, B - 2), None)

        @block.scalar
        def _(act):
            act.wait_ge(consts_in, 16 * (2 + len(ROWS)))
            iu = KT * PCOLS.index("L0_xattn_b_u")
            nc.scalar.mul(half_b[:, :], pp[:, iu:iu + 2 * KT], 0.5).then_inc(half_b_ready, 1)
            act.wait_ge(half_b_ready, 1)
            for n in range(EARLY):
                weights_hi(act, n)
            def hi_xT(it):
                act.wait_ge(z["xT"], it + 1)
                if not (isinstance(it, int) and it == 0):
                    act.wait_ge(z["xT_full"], it)
                for kt in range(KT):
                    last = nc.scalar.copy(xTh[:, kt, :], bank[kt][:, :])
                last.then_inc(z["xT_hi"], 1)

            def hi_context(it):
                act.wait_ge(z["cT"], it + 1)
                nc.scalar.copy(cTh[:, :, :], first_c()).then_inc(z["cT_hi"], 1)

            def hi_tokens(it):
                act.wait_ge(z["tokT"], it + 1)
                for m in range(KT):
                    last = nc.scalar.activation(tTh[:, m, :], first_tokT()[:, m, :], ACT.Identity,
                                                bias=pcol("L0_xattn_b_proj", m))
                last.then_inc(z["tokT_hi"], 1)
                act.wait_ge(z["tok_full"], it + 1)
                nc.scalar.copy(tkh[:, :, :], tkf[:, :, :]).then_inc(z["tok_hi"], 1)

            def softmax_first(it):
                act.wait_ge(z["negmax"], 2 * (it + 1))
                for t in range(L0T):
                    last = nc.scalar.activation(p0[:, t, :], bank[0][:, t * 128:t * 128 + SC], ACT.Exp,
                                                bias=nms0[:, t:t + 1], scale=D ** -0.5, accum_out=sum0[:, t:t + 1])
                last.then_inc(z["exp"], 1)
                act.wait_ge(z["pT"], it + 1)
                nc.scalar.copy(pTh0[:, :], bank[2][0:SC, :]).then_inc(z["pT_hi"], 1)

            def first_layer(it, front):
                act.wait_ge(z["ps_full"], it + 1)
                nc.scalar.copy(psh[:, :, :], psf[:, :, :]).then_inc(z["ps_hi"], 1)
                if front:
                    hi_xT(it + 1)
                act.wait_ge(z["in_full"], it + 1)
                nc.scalar.copy(inh[:, :, :], inf[:, :, :]).then_inc(z["in_hi"], 1)
                if front:
                    hi_context(it + 1)
                    hi_tokens(it + 1)
                for m in range(KT):
                    act.wait_ge(z["gate_r"], it * KT + m + 1)
                    nc.scalar.activation(tr[:, m, :], bank[6 + m][:, :], ACT.Tanh, bias=half_b[:, KT + m:KT + m + 1],
                                         scale=0.5).then_inc(z["tanh_r"], 1)
                for m in range(KT):
                    act.wait_ge(z["rps"], it * KT + m + 1)
                    nc.scalar.mul(rph[:, m, :], tr[:, m, :], 0.5).then_inc(z["rps_hi"], 1)
                for m in range(KT):
                    act.wait_ge(z["gate_u"], it * KT + m + 1)
                    nc.scalar.activation(tu[:, m, :], bank[5 - 2 * m][:, :], ACT.Tanh, bias=half_b[:, m:m + 1],
                                         scale=0.5).then_inc(z["tanh_u"], 1)
                if front:
                    softmax_first(it + 1)
                for m in range(KT):
                    act.wait_ge(z["gate_n"], it * KT + m + 1)
                    nc.scalar.activation(cand[:, m, :], bank[1 + 3 * m][:, :], ACT.Tanh,
                                         bias=pcol("L0_xattn_b_n", m)).then_inc(z["cand"], 1)

            hi_xT(0)
            hi_context(0)
            hi_tokens(0)
            softmax_first(0)
            first_layer(0, True)
            with act.Fori(0, NI - 2) as i:
                first_layer(i + 1, True)
            first_layer(NI - 1, False)

            def prepare(ph, it, read=None):
                act.wait_ge(ph.sem["h_full"], (it + 1) * KT)
                if read:
                    act.wait_ge(*read)
                nc.scalar.copy(hh[:, :, :], hf[:, :, :]).then_inc(ph.sem["h_hi"], 1)

            def prepare_context(it):
                act.wait_ge(a2["cT"], it + 1)
                nc.scalar.copy(ch[:, :, :], c_src()).then_inc(a2["cT_hi"], 1)

            def softmax_pair(ph, it, g):
                a, cols = ph.sem, ph.cols
                for e in range(2):
                    per = 2 if cols == S else 1
                    act.wait_ge(a["negmax"], (it * PAIRS + g) * per + min(e + 1, per))
                    for t in range(NT):
                        last = nc.scalar.activation(p[:, g % 2, e, t * cols:(t + 1) * cols],
                                                    scores_at(cols, g, e, t), ACT.Exp,
                                                    bias=negmax[:, g % 2, t, e:e + 1],
                                                    accum_out=expsum[:, g % 2, t, e:e + 1])
                    last.then_inc(a["exp"], 1)

            def round_pT(ph, it, g):
                r, n = (128, NT * S) if ph.cols == S else (SC, S)
                for e in range(2):
                    act.wait_ge(ph.sem["pT"], it * HEADS + 2 * g + e + 1)
                    nc.scalar.copy(pTh[0:r, g % 2, e, 0:n], bank[4 + e][0:r, 0:n]).then_inc(ph.sem["pT_hi"], 1)

            def copy_rT(ph, it, g):
                act.wait_ge(ph.sem["o"], it * PAIRS + g + 1)
                nc.scalar.copy(rT[:, :], bank[6][:, S:2 * S]).then_inc(ph.sem["rT_copied"], 1)

            def project(ph, it, prev):
                a = ph.sem
                if ph is A1:
                    for g in range(PAIRS):
                        act.wait_ge(a["qk"], it * PAIRS + g + 1)
                        nc.scalar.copy(qkh[:, g, :, :], bank[g % 4][:, :].rearrange("p (a n) -> p a n", a=2)
                                       ).then_inc(a["qk_hi"], 1)
                        if g == 1 and prev:
                            copy_rT(*prev, PAIRS - 1)
                else:
                    for c in range(2):
                        act.wait_ge(a["qk"], it * 6 + c + 1)
                        for e in range(2):
                            last = nc.scalar.copy(k_dst(kdh, c, e), k_src(c, e))
                        last.then_inc(a["qk_hi"], 1)
                        if c == 0:
                            copy_rT(*prev, PAIRS - 1)
                    for c in range(4):
                        act.wait_ge(a["qk"], it * 6 + 3 + c)
                        nc.scalar.copy(qkh[:, 2 * c:2 * c + 2, 0, :], q_src(c)).then_inc(a["qk_hi"], 1)
                softmax_pair(ph, it, 0)
                nv, r = (4, 128) if ph is A1 else (2, SC)
                for c in range(nv):
                    act.wait_ge(a["v"], it * nv + c + 1)
                    nc.scalar.copy(v_dst(vh, r, c), v_src(r, c)).then_inc(a["v_hi"], 1)

            def attention(ph, it, prev, nxt):
                project(ph, it, prev)
                if prev and prev[0] is A1 and ph is A2:
                    for n in (AT_A2, AT_A2 + 1):
                        act.wait_ge(a1["out"], B)
                        weights_hi(act, n)
                for s in range(PAIRS):
                    round_pT(ph, it, s)
                    if s + 1 < PAIRS:
                        softmax_pair(ph, it, s + 1)
                    if s >= 1:
                        copy_rT(ph, it, s - 1)
                    if nxt[0] is not ph and 1 <= s <= 6:
                        weights_hi(act, (AT_A1 if ph is A1 else AT_A2_WO) + s - 1)
                    if nxt[0] is A2 and s == 2:
                        prepare_context(nxt[1])
                    if s == 6:
                        prepare(*nxt)

            def feed_forward(it, prev, nxt):
                for j in range(FF // 128):
                    act.wait_ge(f3["up"], it * 8 + j + 1)
                    if j >= 2:
                        act.wait_ge(f3["glu"], it * 8 + j - 1)
                    nc.scalar.activation(gl[:, j % 2, :], bank[j % 4][:, S:2 * S], ACT.Gelu,
                                         bias=pp[:, NPC - 8 + j:NPC - 7 + j]).then_inc(f3["gelu"], 1)
                    if j >= 1:
                        round_f(it, j - 1)
                    if j == 1 and prev and prev[0] is A2:
                        copy_rT(*prev, PAIRS - 1)
                round_f(it, FF // 128 - 1)
                if nxt:
                    prepare(*nxt, read=(f3["up"], it * 8 + 8))

            def round_f(it, j):
                act.wait_ge(f3["glu"], it * 8 + j + 1)
                nc.scalar.copy(fh[:, j, :], fu[:, j % 2, :]).then_inc(f3["f_hi"], 1)

            act.wait_ge(z["out"], NI)
            for n in range(EARLY, AT_A1):
                weights_hi(act, n)
            prepare(A1, 0)
            attention(A1, 0, None, (A1, 1))
            with act.Fori(0, B - 2) as i:
                attention(A1, i + 1, (A1, i), (A1, i + 2))
            attention(A1, B - 1, (A1, B - 2), (A2, 0))
            attention(A2, 0, (A1, B - 1), (A2, 1))
            with act.Fori(0, B - 2) as i:
                attention(A2, i + 1, (A2, i), (A2, i + 2))
            attention(A2, B - 1, (A2, B - 2), (FFN, 0))
            feed_forward(0, (A2, B - 1), (FFN, 1))
            with act.Fori(0, B - 2) as i:
                feed_forward(i + 1, None, (FFN, i + 2))
            feed_forward(B - 1, None, None)

        @block.vector
        def _(dve):
            dve.wait_ge(consts_in, 16 * (2 + len(ROWS)))
            for n in range(EARLY):
                weights_lo(dve, n)

            def statistics(src, dst, n, sm, base):
                for t in range(n):
                    nc.vector.bn_stats(st6[:, t, :], src(t)).then_inc(sm, 1)
                dve.wait_ge(sm, base + n)
                apart(dve)
                for t in range(n):
                    nc.vector.bn_aggr(dst[:, t, :], st6[:, t, :]).then_inc(sm, 1)
                dve.wait_ge(sm, base + 2 * n)
                for t in range(n):
                    nc.vector.tensor_scalar(dst[:, t, 1:2], dst[:, t, 1:2], EPS, None, ALU.add).then_inc(sm, 1)

            def normalise(dst, src, stat, inv, n, done):
                for t in range(n):
                    nc.vector.tensor_scalar(dst(t), src(t), stat[:, t, 0:1], inv[:, t:t + 1],
                                            ALU.subtract, ALU.mult).then_inc(done, 1)

            def lo_xT(it):
                dve.wait_ge(z["xT_hi"], it + 1)
                for kt in range(KT):
                    last = nc.vector.tensor_tensor(xTl[:, kt, :], bank[kt][:, :], xTh[:, kt, :].bitcast(F32),
                                                   ALU.subtract)
                last.then_inc(z["xT_split"], 1)

            def lo_context(it):
                dve.wait_ge(z["cT_hi"], it + 1)
                nc.vector.tensor_tensor(cTl[:, :, :], first_c(), cTh[:, :, :].bitcast(F32),
                                        ALU.subtract).then_inc(z["cT_split"], 1)

            def normalise_state(it):
                dve.wait_ge(z["in"], 32 * (it + 1))
                statistics(lambda t: x0[:, t, :], mv, L0T, z["stats"], it * 3 * L0T)
                dve.wait_ge(z["rstd"], it + 1)
                normalise(lambda t: xh0[:, t, :], lambda t: x0[:, t, :], mv, rstd, L0T, z["xhat"])

            def lo_tokens(it):
                dve.wait_ge(z["tokT_hi"], it + 1)
                for m in range(KT):
                    last = nc.vector.scalar_tensor_tensor(out=tTl[:, m, :], in0=first_tokT()[:, m, :],
                                                          scalar=pcol("L0_xattn_b_proj", m),
                                                          in1=tTh[:, m, :].bitcast(F32), op0=ALU.add, op1=ALU.subtract)
                last.then_inc(z["tokT_split"], 1)
                dve.wait_ge(z["tok"], it + 1)
                nc.vector.tensor_tensor(tkf[:, :, :], bank[2][0:SC, :].rearrange("p (b n) -> p b n", b=L0B),
                                        row("L0_xattn_b_proj")[0:SC].unsqueeze(1).broadcast_to([SC, L0B, D]),
                                        ALU.add).then_inc(z["tok_full"], 1)

            def max_first(it):
                dve.wait_ge(z["scores"], it + 1)
                nc.vector.tensor_reduce(nm0[:, :], bank[0][:, :].rearrange("p (t n) -> p t n", t=L0T)[:, :, 0:SC],
                                        AX.X, ALU.max, negate=True).then_inc(z["negmax"], 1)
                dve.wait_ge(z["negmax"], 2 * it + 1)
                nc.vector.tensor_scalar(nms0[:, :], nm0[:, :], D ** -0.5, None, ALU.mult).then_inc(z["negmax"], 1)
                dve.wait_ge(z["tok_hi"], it + 1)
                nc.vector.tensor_tensor(tkl[:, :, :], tkf[:, :, :], tkh[:, :, :].bitcast(F32),
                                        ALU.subtract).then_inc(z["tok_split"], 1)

            def lo_p(it):
                dve.wait_ge(z["exp"], it + 1)
                nc.vector.reciprocal(rs0[:, :], sum0[:, :]).then_inc(z["rsum"], 1)
                dve.wait_ge(z["pT_hi"], it + 1)
                nc.vector.tensor_tensor(pTl0[:, :], bank[2][0:SC, :], pTh0[:, :].bitcast(F32),
                                        ALU.subtract).then_inc(z["pT_split"], 1)

            def normalise_routed(it):
                dve.wait_ge(z["rsum"], it + 1)
                dve.wait_ge(z["routed"], it + 1)
                for t in range(L0T):
                    nc.vector.tensor_scalar(rt[:, t, :], bank[t // 2 * 7][:, t % 2 * D:(t % 2 + 1) * D],
                                            rs0[:, t:t + 1], None, ALU.mult).then_inc(z["rt"], 1)
                dve.wait_ge(z["rt"], L0T * (it + 1))
                statistics(lambda t: rt[:, t, :], mv2, L0T, z["rstats"], it * 3 * L0T)
                dve.wait_ge(z["rrstd"], it + 1)
                normalise(lambda t: rt[:, t, :], lambda t: rt[:, t, :], mv2, rstd2, L0T, z["rhat"])

            def first_layer(it, front):
                dve.wait_ge(z["psT"], it + 1)
                for kt in range(KT):
                    last = nc.vector.tensor_scalar(psf[:, kt, :], bank[6 + kt][:, :], pcol("L0_xattn_g_state", kt),
                                                   pcol("L0_xattn_beta_state", kt), ALU.mult, ALU.add)
                last.then_inc(z["ps_full"], 1)
                dve.wait_ge(z["ps_hi"], it + 1)
                nc.vector.tensor_tensor(psl[:, :, :], psf[:, :, :], psh[:, :, :].bitcast(F32),
                                        ALU.subtract).then_inc(z["ps_split"], 1)
                if front:
                    lo_xT(it + 1)
                dve.wait_ge(z["inT"], it + 1)
                for kt in range(KT):
                    last = nc.vector.tensor_scalar(inf[:, kt, :], bank[3 + kt][:, :], pcol("L0_xattn_g_input", kt),
                                                   pcol("L0_xattn_beta_input", kt), ALU.mult, ALU.add)
                last.then_inc(z["in_full"], 1)
                dve.wait_ge(z["in_hi"], it + 1)
                nc.vector.tensor_tensor(inl[:, :, :], inf[:, :, :], inh[:, :, :].bitcast(F32),
                                        ALU.subtract).then_inc(z["in_split"], 1)
                if front:
                    lo_context(it + 1)
                    normalise_state(it + 1)
                    lo_tokens(it + 1)
                for m in range(KT):
                    dve.wait_ge(z["tanh_r"], it * KT + m + 1)
                    nc.vector.scalar_tensor_tensor(out=tr[:, m, :], in0=tr[:, m, :], scalar=1.0, in1=psf[:, m, :],
                                                   op0=ALU.add, op1=ALU.mult).then_inc(z["rps"], 1)
                for m in range(KT):
                    dve.wait_ge(z["rps_hi"], it * KT + m + 1)
                    nc.vector.scalar_tensor_tensor(out=rpl[:, m, :], in0=tr[:, m, :], scalar=0.5,
                                                   in1=rph[:, m, :].bitcast(F32), op0=ALU.mult,
                                                   op1=ALU.subtract).then_inc(z["rps_split"], 1)
                if front:
                    max_first(it + 1)
                    lo_p(it + 1)
                dve.wait_ge(z["xT_full"], it + 1)
                for m in range(KT):
                    dve.wait_ge(z["cand"], it * KT + m + 1)
                    nc.vector.tensor_tensor(cand[:, m, :], cand[:, m, :], xTf[:, m, :], ALU.subtract
                                            ).then_inc(z["new_step"], 1)
                for m in range(KT):
                    dve.wait_ge(z["tanh_u"], it * KT + m + 1)
                    dve.wait_ge(z["new_step"], it * 4 + m + 1)
                    nc.vector.scalar_tensor_tensor(out=cand[:, m, :], in0=tu[:, m, :], scalar=1.0, in1=cand[:, m, :],
                                                   op0=ALU.add, op1=ALU.mult).then_inc(z["new_step"], 1)
                for m in range(KT):
                    dve.wait_ge(z["new_step"], it * 4 + 3 + m)
                    nc.vector.scalar_tensor_tensor(out=cand[:, m, :], in0=cand[:, m, :], scalar=0.5, in1=xTf[:, m, :],
                                                   op0=ALU.mult, op1=ALU.add).then_inc(z["new"], 1)
                if front:
                    normalise_routed(it + 1)
                dve.wait_ge(z["new_tok"], it + 1)
                new_at = lambda t: bank[5 - t // 2 * 3][:, t % 2 * D:(t % 2 + 1) * D]
                statistics(new_at, mv, L0T, z["ostats"], it * 3 * L0T)
                dve.wait_ge(z["orstd"], it + 1)
                dve.wait_ge(z["stored"], 16 * (it + 1))
                normalise(lambda t: x1o[:, t, :], new_at, mv, rstd, L0T, z["ohat"])
                dve.wait_ge(z["ohat"], it * (L0T + 1) + L0T)
                nc.vector.tensor_tensor(x1o[:, :, :], x1o[:, :, :],
                                        row("L0_xattn_g_out").unsqueeze(1).broadcast_to([128, L0T, D]),
                                        ALU.mult).then_inc(z["ohat"], 1)
                dve.wait_ge(z["ohat"], (it + 1) * (L0T + 1))
                nc.vector.tensor_tensor(x1o[:, :, :], x1o[:, :, :],
                                        row("L0_xattn_beta_out").unsqueeze(1).broadcast_to([128, L0T, D]),
                                        ALU.add).then_inc(z["out"], 1)

            normalise_state(0)
            lo_xT(0)
            lo_context(0)
            lo_tokens(0)
            max_first(0)
            lo_p(0)
            normalise_routed(0)
            first_layer(0, True)
            with dve.Fori(0, NI - 2) as i:
                first_layer(i + 1, True)
            first_layer(NI - 1, False)

            def prepare_stats(ph, it):
                dve.wait_ge(ph.sem["in"], 16 * (it + 1))
                statistics(lambda t: xin[:, t, :], mv, NT, ph.sem["stats"], it * 3 * NT)

            def prepare_xhat(ph, it):
                dve.wait_ge(ph.sem["rstd"], it + 1)
                normalise(lambda t: xhat[:, t, :], lambda t: xin[:, t, :], mv, rstd, NT, ph.sem["xhat"])

            def prepare_full(ph, it, bk):
                dve.wait_ge(ph.sem["hT"], it + 1)
                for kt in range(KT):
                    nc.vector.tensor_scalar(hf[:, kt, :], bank[bk][:, kt * S:(kt + 1) * S], pcol(ph.gamma, kt),
                                            pcol(ph.beta, kt), ALU.mult, ALU.add).then_inc(ph.sem["h_full"], 1)

            def prepare_lo(ph, it):
                dve.wait_ge(ph.sem["h_hi"], it + 1)
                nc.vector.tensor_tensor(hl[:, :, :], hf[:, :, :], hh[:, :, :].bitcast(F32),
                                        ALU.subtract).then_inc(ph.sem["h_split"], 1)

            def prepare_context(it):
                dve.wait_ge(a2["cT_hi"], it + 1)
                nc.vector.tensor_tensor(cl[:, :, :], c_src(), ch[:, :, :].bitcast(F32),
                                        ALU.subtract).then_inc(a2["cT_lo"], 1)

            def row_max(ph, it, g):
                a = ph.sem
                dve.wait_ge(a["scores"], it * PAIRS + g + 1)
                if ph.cols == S:
                    for e in range(2):
                        nc.vector.tensor_reduce(negmax[:, g % 2, :, e],
                                                bank[g % 2 * 2 + e][:, :].rearrange("p (t n) -> p t n", t=NT),
                                                AX.X, ALU.max, negate=True).then_inc(a["negmax"], 1)
                else:
                    nc.vector.tensor_reduce(
                        negmax[:, g % 2, :, :],
                        bank[g % 4][:, :].rearrange("p (t n) -> p t n", t=NT)[:, :, 0:2 * SC]
                        .rearrange("p t (e n) -> p t e n", e=2), AX.X, ALU.max, negate=True
                    ).then_inc(a["negmax"], 1)

            def inverse_sums(ph, it, g):
                dve.wait_ge(ph.sem["exp"], it * HEADS + 2 * g + 2)
                nc.vector.reciprocal(rs[:, g % 2, :], expsum[:, g % 2, :, :].rearrange("p t e -> p (t e)")
                                     ).then_inc(ph.sem["rsum"], 1)
                dve.wait_ge(ph.sem["rsum"], 2 * (it * PAIRS + g) + 1)
                nc.vector.tensor_copy(rsw[:, g % 2, :, :].rearrange("p t (e d) -> p (t e) d", e=2),
                                      rs[:, g % 2, :].unsqueeze(2).broadcast_to([128, NT * 2, DH])
                                      ).then_inc(ph.sem["rsum"], 1)

            def pT_low(ph, it, g):
                r, n = (128, NT * S) if ph.cols == S else (SC, S)
                for e in range(2):
                    dve.wait_ge(ph.sem["pT_hi"], it * HEADS + 2 * g + e + 1)
                    nc.vector.tensor_tensor(pTl[0:r, g % 2, e, 0:n], bank[4 + e][0:r, 0:n],
                                            pTh[0:r, g % 2, e, 0:n].bitcast(F32),
                                            ALU.subtract).then_inc(ph.sem["pT_lo"], 1)

            def normalise_o(ph, it, g):
                dve.wait_ge(ph.sem["rT_copied"], it * PAIRS + g + 1)
                if g >= 1:
                    dve.wait_ge(ph.sem["o_lo"], it * PAIRS + g)
                nc.vector.tensor_tensor(of[:, :], bank[6][:, 0:S], rT[:, :], ALU.mult).then_inc(ph.sem["o_norm"], 1)

            def residual(ph, it, first):
                a = ph.sem
                dve.wait_ge(a["xb"], it + 1)
                dve.wait_ge(a["stored"], 16 * (it + 1))
                if first and ph is not A1:
                    dve.wait_ge((a1 if ph is A2 else a2)["stored"], 16 * (B + 1))
                if ph is FFN:
                    dve.wait_ge(a["down"], it + 1)
                else:
                    dve.wait_ge(a["wo"], (it + 1) * PAIRS)
                for t in range(NT):
                    last = nc.vector.tensor_tensor(xo[:, t, :], bank[7 - t][:, 0:D], xb[:, t, :], ALU.add)
                last.then_inc(a["out"], 1)

            def project(ph, it, prev):
                a = ph.sem
                if ph is A1:
                    for g in range(PAIRS):
                        dve.wait_ge(a["qk_hi"], it * PAIRS + g + 1)
                        nc.vector.tensor_tensor(qkl[:, g, :, :], bank[g % 4][:, :].rearrange("p (a n) -> p a n", a=2),
                                                qkh[:, g, :, :].bitcast(F32), ALU.subtract).then_inc(a["qk_lo"], 1)
                        if g == 1 and prev:
                            normalise_o(*prev[0:2], PAIRS - 1)
                else:
                    for c in range(2):
                        dve.wait_ge(a["qk_hi"], it * 6 + c + 1)
                        for e in range(2):
                            last = nc.vector.tensor_tensor(k_dst(kdl, c, e), k_src(c, e),
                                                           k_dst(kdh, c, e).bitcast(F32), ALU.subtract)
                        last.then_inc(a["qk_lo"], 1)
                        if c == 0:
                            normalise_o(*prev[0:2], PAIRS - 1)
                    for c in range(4):
                        dve.wait_ge(a["qk_hi"], it * 6 + 3 + c)
                        nc.vector.tensor_tensor(qkl[:, 2 * c:2 * c + 2, 0, :], q_src(c),
                                                qkh[:, 2 * c:2 * c + 2, 0, :].bitcast(F32),
                                                ALU.subtract).then_inc(a["qk_lo"], 1)
                row_max(ph, it, 0)
                if prev:
                    residual(*prev)
                nv, r = (4, 128) if ph is A1 else (2, SC)
                for c in range(nv):
                    dve.wait_ge(a["v_hi"], it * nv + c + 1)
                    nc.vector.tensor_tensor(v_dst(vl, r, c), v_src(r, c), v_dst(vh, r, c).bitcast(F32),
                                            ALU.subtract).then_inc(a["v_lo"], 1)

            def attention(ph, it, prev, nxt):
                project(ph, it, prev)
                if prev and prev[0] is A1 and ph is A2:
                    for n in (AT_A2, AT_A2 + 1):
                        weights_lo(dve, n)
                row_max(ph, it, 1)
                for s in range(PAIRS):
                    inverse_sums(ph, it, s)
                    pT_low(ph, it, s)
                    if s + 2 < PAIRS:
                        row_max(ph, it, s + 2)
                    if s >= 1:
                        normalise_o(ph, it, s - 1)
                    if nxt[0] is not ph and 1 <= s <= 6:
                        weights_lo(dve, (AT_A1 if ph is A1 else AT_A2_WO) + s - 1)
                    if s == 2:
                        prepare_stats(*nxt)
                    if s == 3:
                        prepare_xhat(*nxt)
                        if nxt[0] is A2:
                            prepare_context(nxt[1])
                    if s == 5:
                        prepare_full(*nxt, 7)
                    if s == 6:
                        prepare_lo(*nxt)

            def f_low(it, j):
                dve.wait_ge(f3["f_hi"], it * 8 + j + 1)
                nc.vector.tensor_tensor(fl[:, j, :], fu[:, j % 2, :], fh[:, j, :].bitcast(F32),
                                        ALU.subtract).then_inc(f3["f_lo"], 1)

            def feed_forward(it, prev, nxt):
                for j in range(FF // 128):
                    dve.wait_ge(f3["gelu"], it * 8 + j + 1)
                    if j >= 2:
                        dve.wait_ge(f3["f_lo"], it * 8 + j - 1)
                    nc.vector.scalar_tensor_tensor(out=fu[:, j % 2, :], in0=bank[j % 4][:, 0:S],
                                                   scalar=pp[:, NPC - 16 + j:NPC - 15 + j], in1=gl[:, j % 2, :],
                                                   op0=ALU.add, op1=ALU.mult).then_inc(f3["glu"], 1)
                    if j >= 1:
                        f_low(it, j - 1)
                    if prev:
                        if j == 1:
                            normalise_o(*prev[0:2], PAIRS - 1)
                        if j == 3:
                            residual(*prev)
                    if nxt:
                        if j == 3:
                            prepare_stats(*nxt)
                        if j == 4:
                            prepare_xhat(*nxt)
                        if j == 7:
                            prepare_full(*nxt, 4)
                f_low(it, FF // 128 - 1)
                if nxt:
                    prepare_lo(*nxt)
                residual(FFN, it, isinstance(it, int) and it == 0)

            dve.wait_ge(z["out"], NI)
            for n in range(EARLY, AT_A1):
                weights_lo(dve, n)
            for v_ in (vh, vl):
                for pr in range(PAIRS):
                    last = nc.vector.memset(v_[:, :, pr * VW + DH:pr * VW + 2 * DH].bitcast(F32), 0.0)
            last.then_inc(zeros_ready, 1)
            prepare_stats(A1, 0)
            prepare_xhat(A1, 0)
            prepare_full(A1, 0, 7)
            prepare_lo(A1, 0)
            attention(A1, 0, None, (A1, 1))
            with dve.Fori(0, B - 2) as i:
                attention(A1, i + 1, (A1, i, False), (A1, i + 2))
            attention(A1, B - 1, (A1, B - 2, False), (A2, 0))
            for k_ in (kdh, kdl):
                nc.vector.memset(k_[0:DH, :, SC:2 * SC].bitcast(F32), 0.0)
                last = nc.vector.memset(k_[DH:128, :, 0:SC].bitcast(F32), 0.0)
            last.then_inc(zeros_ready, 1)
            attention(A2, 0, (A1, B - 1, False), (A2, 1))
            with dve.Fori(0, B - 2) as i:
                attention(A2, i + 1, (A2, i, False), (A2, i + 2))
            attention(A2, B - 1, (A2, B - 2, False), (FFN, 0))
            feed_forward(0, (A2, B - 1, False), (FFN, 1))
            with dve.Fori(0, B - 2) as i:
                feed_forward(i + 1, None, (FFN, i + 2))
            feed_forward(B - 1, None, None)

        @block.tensor
        def _(pe):
            def product(dst, terms):
                n = len(terms)
                for i, ((lh, ll), (rh, rl)) in enumerate(terms):
                    nc.tensor.matmul(dst, lh, rh, start=(i == 0), stop=False)
                    nc.tensor.matmul(dst, lh, rl, start=False, stop=False)
                    last = nc.tensor.matmul(dst, ll, rh, start=False, stop=(i == n - 1))
                return last

            pe.wait_ge(consts_in, 16 * (2 + len(ROWS)))
            pe.wait_ge(w_ready, WCHUNKS[0])
            def first_xT(it):
                pe.wait_ge(z["in"], 32 * (it + 1))
                for t in range(L0T):
                    for kt in range(KT):
                        last = nc.tensor.transpose(bank[kt][:, t * 128:(t + 1) * 128],
                                                   x0[:, t, kt * 128:(kt + 1) * 128], ident[:, :])
                last.then_inc(z["xT"], 1)

            def first_cT(it):
                for c in range(L0B):
                    for kt in range(KT):
                        last = nc.tensor.transpose(bank[2][:, kt * 256 + c * SC:kt * 256 + (c + 1) * SC],
                                                   c0[:, c, kt * 128:(kt + 1) * 128], ident[0:SC, 0:SC])
                last.then_inc(z["cT"], 1)

            def first_tokens(it):
                pe.wait_ge(z["cT_split"], it + 1)
                for m in range(KT):
                    last = product(bank[4][:, m * 256:m * 256 + L0B * SC],
                                   [(wcols(0, "L0_xattn_W_proj", kt, m * 128, 128), (cTh[:, kt, :], cTl[:, kt, :]))
                                    for kt in range(KT)])
                last.then_inc(z["tokT"], 1)
                for c in range(L0B):
                    cc = slice(c * SC, (c + 1) * SC)
                    last = product(bank[2][0:SC, c * D:(c + 1) * D],
                                   [((cTh[:, kt, cc], cTl[:, kt, cc]), wcols(0, "L0_xattn_W_proj", kt, 0, D))
                                    for kt in range(KT)])
                last.then_inc(z["tok"], 1)

            def first_scores(it):
                pe.wait_ge(z["xT_split"], it + 1)
                pe.wait_ge(z["tokT_split"], it + 1)
                for t in range(L0T):
                    tt, cc = slice(t * 128, (t + 1) * 128), slice(t // NT * SC, (t // NT + 1) * SC)
                    last = product(bank[0][:, t * 128:t * 128 + SC],
                                   [((xTh[:, kt, tt], xTl[:, kt, tt]), (tTh[:, kt, cc], tTl[:, kt, cc]))
                                    for kt in range(KT)])
                last.then_inc(z["scores"], 1)

            def first_pT(it):
                pe.wait_ge(z["exp"], it + 1)
                pe.wait_ge(z["tok_split"], it + 1)
                for t in range(L0T):
                    last = nc.tensor.transpose(bank[2][0:SC, t * 128:(t + 1) * 128], p0[:, t, :], ident[:, :])
                last.then_inc(z["pT"], 1)

            def first_routed(it):
                pe.wait_ge(z["pT_split"], it + 1)
                for t in range(L0T):
                    tt = slice(t * 128, (t + 1) * 128)
                    last = product(bank[t // 2 * 7][:, t % 2 * D:(t % 2 + 1) * D],
                                   [((pTh0[:, tt], pTl0[:, tt]), (tkh[:, t // NT, :], tkl[:, t // NT, :]))])
                last.then_inc(z["routed"], 1)

            def gate_part(dst, name, m, k0, part, start, stop):
                for kt in range(KT):
                    wh, wl = wcols(0, name, k0 + kt, m * 128, 128)
                    nc.tensor.matmul(dst, wh, part[0][:, kt, :], start=start and kt == 0, stop=False)
                    nc.tensor.matmul(dst, wh, part[1][:, kt, :], start=False, stop=False)
                    last = nc.tensor.matmul(dst, wl, part[0][:, kt, :], start=False, stop=stop and kt == KT - 1)
                return last

            def first_layer(it, front, first=False):
                pe.wait_ge(z["xhat"], L0T * (it + 1))
                pe.wait_ge(z["rt"], L0T * (it + 1))
                for t in range(L0T):
                    for kt in range(KT):
                        last = nc.tensor.transpose(bank[6 + kt][:, t * 128:(t + 1) * 128],
                                                   xh0[:, t, kt * 128:(kt + 1) * 128], ident[:, :])
                last.then_inc(z["psT"], 1)
                if front:
                    first_xT(it + 1)
                pe.wait_ge(z["rhat"], L0T * (it + 1))
                for t in range(L0T):
                    for kt in range(KT):
                        last = nc.tensor.transpose(bank[3 + kt][:, t * 128:(t + 1) * 128],
                                                   rt[:, t, kt * 128:(kt + 1) * 128], ident[:, :])
                last.then_inc(z["inT"], 1)
                if not first:
                    pe.wait_ge(z["ohat"], it * (L0T + 1) - 1)
                if front:
                    first_cT(it + 1)
                pe.wait_ge(z["ps_split"], it + 1)
                state, routed, reset = (psh, psl), (inh, inl), (rph, rpl)
                r_u = [(6, "L0_xattn_W_r", 0), (7, "L0_xattn_W_r", 1), (5, "L0_xattn_W_u", 0), (3, "L0_xattn_W_u", 1)]
                for b, name, m in r_u:
                    if b == 3:
                        pe.wait_ge(z["in_full"], it + 1)
                    gate_part(bank[b][:, :], name, m, 0, state, True, False)
                if front:
                    first_tokens(it + 1)
                pe.wait_ge(z["in_split"], it + 1)
                for b, name, m in r_u:
                    gate_part(bank[b][:, :], name, m, 2, routed, False, True).then_inc(
                        z["gate_r" if name == "L0_xattn_W_r" else "gate_u"], 1)
                if front:
                    first_scores(it + 1)
                for m in range(KT):
                    gate_part(bank[1 + 3 * m][:, :], "L0_xattn_W_n", m, 2, routed, True, False)
                if front:
                    first_pT(it + 1)
                pe.wait_ge(z["rps_split"], KT * (it + 1))
                for m in range(KT):
                    gate_part(bank[1 + 3 * m][:, :], "L0_xattn_W_n", m, 0, reset, False, True).then_inc(z["gate_n"], 1)
                if front:
                    first_routed(it + 1)
                pe.wait_ge(z["new"], KT * (it + 1))
                for t in range(L0T):
                    for kt in range(KT):
                        last = nc.tensor.transpose(
                            bank[5 - t // 2 * 3][:, t % 2 * D + kt * 128:t % 2 * D + (kt + 1) * 128],
                            cand[:, kt, t * 128:(t + 1) * 128], ident[:, :])
                last.then_inc(z["new_tok"], 1)

            first_xT(0)
            first_cT(0)
            first_tokens(0)
            first_scores(0)
            first_pT(0)
            first_routed(0)
            first_layer(0, True, first=True)
            with pe.Fori(0, NI - 2) as i:
                first_layer(i + 1, True)
            first_layer(NI - 1, False)

            def prepare(ph, it, bk):
                pe.wait_ge(ph.sem["xhat"], NT * (it + 1))
                for t in range(NT):
                    for kt in range(KT):
                        last = nc.tensor.transpose(bank[bk][:, kt * S + t * 128:kt * S + (t + 1) * 128],
                                                   xhat[:, t, kt * 128:(kt + 1) * 128], ident[:, :])
                last.then_inc(ph.sem["hT"], 1)

            def prepare_context(it):
                pe.wait_ge(a2["c_in"], 16 * (it + 1))
                for kt in range(KT):
                    last = nc.tensor.transpose(bank[7][:, kt * 256:kt * 256 + SC], cin[:, kt * 128:(kt + 1) * 128],
                                               ident[0:SC, 0:SC])
                last.then_inc(a2["cT"], 1)

            def scores(ph, it, g):
                if g >= 2:
                    pe.wait_ge(ph.sem["exp"], it * HEADS + 2 * (g - 1))
                for t in range(NT):
                    tt = slice(t * 128, (t + 1) * 128)
                    if ph.cols == S:
                        for n, (lhs, rhs) in enumerate(((qkh, qkh), (qkh, qkl), (qkl, qkh))):
                            for e in range(2):
                                pr = slice(e * DH, (e + 1) * DH)
                                last = nc.tensor.matmul(bank[g % 2 * 2 + e][:, t * S:(t + 1) * S],
                                                        lhs[pr, g, 0, tt], rhs[pr, g, 1, :],
                                                        start=(n == 0), stop=(n == 2))
                    else:
                        last = product(bank[g % 4][:, t * S:t * S + 2 * SC],
                                       [((qkh[:, g, 0, tt], qkl[:, g, 0, tt]), (kdh[:, g, :], kdl[:, g, :]))])
                last.then_inc(ph.sem["scores"], 1)

            def transpose_p(ph, it, g):
                cols = ph.cols
                for e in range(2):
                    pe.wait_ge(ph.sem["exp"], it * HEADS + 2 * g + e + 1)
                    if g >= 1:
                        pe.wait_ge(ph.sem["pT_lo"], it * HEADS + 2 * g + e - 1)
                    for t in range(NT):
                        for j in range(NT if cols == S else 1):
                            n = min(cols, 128)
                            last = nc.tensor.transpose(bank[4 + e][0:n, j * S + t * 128:j * S + (t + 1) * 128],
                                                       p[:, g % 2, e, t * cols + j * 128:t * cols + j * 128 + n],
                                                       ident[:, :])
                    last.then_inc(ph.sem["pT"], 1)

            def weighted_values(ph, it, g):
                cols, a = ph.cols, ph.sem
                r = min(cols, 128)
                pe.wait_ge(a["rsum"], 2 * (it * PAIRS + g + 1))
                if g >= 1:
                    pe.wait_ge(a["o_norm"], it * PAIRS + g)
                for t in range(NT):
                    nc.tensor.transpose(bank[6][:, S + t * 128:S + (t + 1) * 128], rsw[:, g % 2, t, :], ident[:, :])
                terms = []
                for e in range(2):
                    for j in range(NT if cols == S else 1):
                        vc = slice(g * VW + e * DH, g * VW + e * DH + 128)
                        pc = slice(j * S, (j + 1) * S)
                        terms.append(((vh[0:r, j, vc], vl[0:r, j, vc]), (pTh[0:r, g % 2, e, pc], pTl[0:r, g % 2, e, pc])))
                pe.wait_ge(a["pT_lo"], it * HEADS + 2 * g + 2)
                product(bank[6][:, 0:S], terms).then_inc(a["o"], 1)

            def project_out(ph, it):
                for g in range(PAIRS):
                    pe.wait_ge(ph.sem["o_lo"], it * PAIRS + g + 1)
                    if g == 0:
                        pe.wait_ge(ph.sem["o_norm"], (it + 1) * PAIRS)
                    for t in range(NT):
                        tt = slice(t * 128, (t + 1) * 128)
                        wh, wl = wcols(ph.n, ph.wo, g, 0, D)
                        dst = bank[7 - t][:, 0:D]
                        nc.tensor.matmul(dst, oh[:, g, tt], wh, start=(g == 0), stop=False)
                        nc.tensor.matmul(dst, oh[:, g, tt], wl, start=False, stop=False)
                        last = nc.tensor.matmul(dst, ol[:, g, tt], wh, start=False, stop=(g == PAIRS - 1))
                    last.then_inc(ph.sem["wo"], 1)

            def project_self(it, prev):
                pe.wait_ge(a1["h_split"], it + 1)
                h = [(hh[:, kt, :], hl[:, kt, :]) for kt in range(KT)]
                for g in range(PAIRS):
                    if g >= 4:
                        pe.wait_ge(a1["qk_lo"], it * PAIRS + g - 3)
                    for i, w in enumerate(("L1_xattn_a1_Wq", "L1_xattn_a1_Wk")):
                        last = product(bank[g % 4][:, i * S:(i + 1) * S],
                                       [(wcols(1, w, kt, g * 128, 128), h[kt]) for kt in range(KT)])
                    last.then_inc(a1["qk"], 1)
                    if g == 1 and prev:
                        weighted_values(*prev, PAIRS - 1)
                pe.wait_ge(a1["qk_lo"], it * PAIRS + 6)
                scores(A1, it, 0)
                if prev:
                    project_out(*prev)
                for c in range(4):
                    if c == 2:
                        pe.wait_ge(a1["qk_lo"], (it + 1) * PAIRS)
                    tt = slice(c // 2 * 128, (c // 2 + 1) * 128)
                    product(bank[(4, 5, 2, 3)[c]][:, :],
                            [((hh[:, kt, tt], hl[:, kt, tt]), wcols(1, "L1_xattn_a1_Wv", kt, c % 2 * 512, 512))
                             for kt in range(KT)]).then_inc(a1["v"], 1)
                pe.wait_ge(a1["v_lo"], (it + 1) * 4)

            def project_cross(it, prev):
                pe.wait_ge(a2["cT_lo"], it + 1)
                cT = [(ch[:, kt, :], cl[:, kt, :]) for kt in range(KT)]
                for c in range(2):
                    for g in range(4):
                        last = product(bank[2 + c][:, g * SC:(g + 1) * SC],
                                       [(wcols(2, "L1_xattn_a2_Wk", kt, (4 * c + g) * 128, 128), cT[kt])
                                        for kt in range(KT)])
                    last.then_inc(a2["qk"], 1)
                    if c == 0:
                        weighted_values(*prev, PAIRS - 1)
                pe.wait_ge(a2["h_split"], it + 1)
                for c in range(4):
                    for g in range(2):
                        last = product(bank[(0, 1, 4, 5)[c]][:, g * S:(g + 1) * S],
                                       [(wcols(2, "L1_xattn_a2_Wq", kt, (2 * c + g) * 128, 128),
                                         (hh[:, kt, :], hl[:, kt, :])) for kt in range(KT)])
                    last.then_inc(a2["qk"], 1)
                pe.wait_ge(a2["qk_lo"], it * 6 + 3)
                scores(A2, it, 0)
                project_out(*prev)
                pe.wait_ge(a2["qk_lo"], (it + 1) * 6)
                for c in range(2):
                    product(bank[4 + c][0:SC, :], [(cT[kt], wcols(2, "L1_xattn_a2_Wv", kt, c * 512, 512))
                                                   for kt in range(KT)]).then_inc(a2["v"], 1)
                pe.wait_ge(a2["v_lo"], (it + 1) * 2)

            def attention(ph, it, prev, nxt):
                if ph is A1:
                    project_self(it, prev)
                else:
                    project_cross(it, prev)
                scores(ph, it, 1)
                if prev:
                    pe.wait_ge(prev[0].sem["out"], prev[1] + 1)
                for s in range(PAIRS):
                    transpose_p(ph, it, s)
                    if s + 2 < PAIRS:
                        scores(ph, it, s + 2)
                    if s >= 1:
                        weighted_values(ph, it, s - 1)
                    if s == 1 and nxt[0] is A2:
                        prepare_context(nxt[1])
                    if s == 4:
                        if nxt[0] is A2:
                            pe.wait_ge(a2["cT_lo"], nxt[1] + 1)
                        prepare(*nxt, 7)

            def feed_forward(it, prev, nxt):
                pe.wait_ge(f3["h_split"], it + 1)
                for j in range(FF // 128):
                    if j >= 4:
                        pe.wait_ge(f3["glu"], it * 8 + j - 3)
                    for i in range(2):
                        last = product(bank[j % 4][:, i * S:(i + 1) * S],
                                       [(wcols(3, "L1_xattn_ff_Wp", kt, i * FF + j * 128, 128),
                                         (hh[:, kt, :], hl[:, kt, :])) for kt in range(KT)])
                    last.then_inc(f3["up"], 1)
                    if j == 1 and prev[0] is A2:
                        weighted_values(*prev, PAIRS - 1)
                    if j == 3:
                        if prev[0] is A2:
                            project_out(*prev)
                        pe.wait_ge(prev[0].sem["out"], prev[1] + 1)
                    if j >= 4:
                        down(it, j - 4)
                    if j == 6 and nxt:
                        prepare(*nxt, 4)
                for j in range(4, FF // 128):
                    down(it, j)

            def down(it, j):
                pe.wait_ge(f3["f_lo"], it * 8 + j + 1)
                for t in range(NT):
                    tt = slice(t * 128, (t + 1) * 128)
                    wh, wl = wcols(3, "L1_xattn_ff_Wo", j, 0, D)
                    dst = bank[7 - t][:, 0:D]
                    nc.tensor.matmul(dst, fh[:, j, tt], wh, start=(j == 0), stop=False)
                    nc.tensor.matmul(dst, fh[:, j, tt], wl, start=False, stop=False)
                    last = nc.tensor.matmul(dst, fl[:, j, tt], wh, start=False, stop=(j == 7))
                if j == 7:
                    last.then_inc(f3["down"], 1)

            pe.wait_ge(z["out"], NI)
            prepare(A1, 0, 7)
            pe.wait_ge(w_ready, AT_A1)
            pe.wait_ge(zeros_ready, 1)
            attention(A1, 0, None, (A1, 1))
            with pe.Fori(0, B - 2) as i:
                attention(A1, i + 1, (A1, i), (A1, i + 2))
            attention(A1, B - 1, (A1, B - 2), (A2, 0))
            pe.wait_ge(w_ready, AT_A2)
            pe.wait_ge(zeros_ready, 2)
            attention(A2, 0, (A1, B - 1), (A2, 1))
            pe.wait_ge(w_ready, AT_A2_WO)
            with pe.Fori(0, B - 2) as i:
                attention(A2, i + 1, (A2, i), (A2, i + 2))
            attention(A2, B - 1, (A2, B - 2), (FFN, 0))
            pe.wait_ge(w_ready, AT_FF)
            feed_forward(0, (A2, B - 1), (FFN, 1))
            with pe.Fori(0, B - 2) as i:
                feed_forward(i + 1, (FFN, i), (FFN, i + 2))
            feed_forward(B - 1, (FFN, B - 2), None)


def kernel(**inputs):
    import numpy as _np
    import concourse.bacc as _bacc
    from concourse import mybir as _mybir
    from concourse.bass_utils import run_bass_kernel_spmd as _run

    a = {k: _np.asarray(v) for k, v in inputs.items()}
    f32 = _np.float32

    def tiles(w):
        k, n = w.shape
        kt = -(-k // 128)
        padded = _np.zeros((kt * 128, n), f32)
        padded[:k] = w
        return padded.reshape(kt, 128, n).transpose(1, 0, 2).reshape(128, kt * n)

    chunks = []
    for ws, n in zip(WSETS, WCHUNKS):
        packed = _np.zeros((128, n * CH), f32)
        at = 0
        for w in ws:
            packed[:, at:at + WIDTH[w]] = tiles(a[w])
            at += WIDTH[w]
        chunks.append(packed.reshape(128, n, CH).transpose(1, 0, 2))
    ctx_padded = _np.zeros((B, SC, D), f32)
    ctx_padded[:, :, :DC] = a["ctx_768"]
    vectors = _np.concatenate([a[n] for n in PCOLS] + [a["L1_xattn_ff_bp"]])
    arrays = {
        "in_x": _np.ascontiguousarray(a["x"]),
        "in_ctx": ctx_padded,
        "in_weights": _np.ascontiguousarray(_np.concatenate(chunks)),
        "in_params": _np.ascontiguousarray(vectors.reshape(NPC, 128).T),
        "in_rows": _np.stack([a[n] for n in ROWS]),
        "in_ident": _np.eye(128, dtype=f32),
    }
    nc = _bacc.Bacc("TRN2", target_bir_lowering=False, num_devices=1)
    aps = [nc.dram_tensor(n, v.shape, _mybir.dt.float32, kind="ExternalInput").ap() for n, v in arrays.items()]
    mid = [nc.dram_tensor(f"x{i}_dram", (B, S, D), _mybir.dt.float32, kind="Internal").ap() for i in (1, 2, 3)]
    out = nc.dram_tensor("out_0_dram", (B, S, D), _mybir.dt.float32, kind="ExternalOutput").ap()
    build(nc, *aps, *mid, out)
    return _run(nc, [arrays], core_ids=[0]).results[0]["out_0_dram"]
```
